# Optimizing a Trainium2 kernel written in Bass

```python
import numpy as np
import jax
import jax.numpy as jnp

def _softmax(x, axis=-1):
    return jax.nn.softmax(x, axis=axis)

def _gelu(x):
    return jax.nn.gelu(x, approximate=True)

def _silu(x):
    return jax.nn.silu(x)

def _sigmoid(x):
    return jax.nn.sigmoid(x)

def _layernorm(x, axis=-1, eps=1e-05):
    m = jnp.mean(x, axis=axis, keepdims=True)
    v = jnp.var(x, axis=axis, keepdims=True)
    return (x - m) / jnp.sqrt(v + eps)

def _scatter_add(tgt, idx, src, axis=0):
    return tgt.at[idx].add(src)

def _segment_sum(src, seg, n):
    return jax.ops.segment_sum(src, seg, n)
kernel_name = 'mk_lm_tower_d2_tok_ids256_r4_e4b89f'

def setup_inputs(seed: int=0):
    np.random.seed(seed)
    _w = jnp.asarray

    def _rec_inputs():
        import jax
        import jax.numpy as jnp
        _rk = jax.random.key(seed)
        x = jax.random.randint(jax.random.fold_in(_rk, 1), (2, 2048), 0, 128, jnp.int32)
        return x
    x = _rec_inputs()

    def _L0_tok_setup():
        import jax, jax.numpy as jnp
        import numpy as np
        VOCAB = 128
        D = 64
        S = 128
        B = 128
        MAX_LEN = 128
        SEP_ID = 13
        PAD_ID = 1

        def _make_pe():
            pos = np.arange(MAX_LEN, dtype=np.float32)[:, None]
            div = np.exp(np.arange(0, D, 2, dtype=np.float32) * (-np.log(10000.0) / D))
            pe = np.zeros((MAX_LEN, D), dtype=np.float32)
            pe[:, 0::2] = np.sin(pos * div)
            pe[:, 1::2] = np.cos(pos * div)
            return jnp.asarray(pe)
        key = jax.random.key(seed)
        k1, k2 = jax.random.split(key)
        sequence = jax.random.randint(k1, (S, B), 0, VOCAB)
        token_W = jax.random.normal(k2, (VOCAB, D), dtype=jnp.float32) * 0.02
        token_W = token_W.at[0].set(0.0)
        pe = _make_pe()
        return {'sequence': sequence, 'token_W': token_W, 'pe': pe}
    _L0_tok_all = _L0_tok_setup()
    _L0_tok_in = {k: v for k, v in _L0_tok_all.items() if k in ('token_W', 'pe')}
    del _L0_tok_all

    def _L0_attn_setup():
        import jax, jax.numpy as jnp
        import numpy as np
        NUM_HEADS = 4
        LN_EPS = 1e-05

        def positional_encoding(length, d_model):
            pos = jnp.arange(length, dtype=jnp.float32)[:, None]
            div = jnp.exp(jnp.arange(0, d_model, 2, dtype=jnp.float32) * (-np.log(10000.0) / d_model))
            pe = jnp.zeros((length, d_model), dtype=jnp.float32)
            pe = pe.at[:, 0::2].set(jnp.sin(pos * div))
            pe = pe.at[:, 1::2].set(jnp.cos(pos * div))
            return pe

        def rel_shift(pos_score):
            B, H, S, _ = pos_score.shape
            padded = jnp.pad(pos_score, ((0, 0), (0, 0), (0, 0), (1, 0)))
            padded = padded.reshape(B, H, S + 1, S)
            return padded[:, :, 1:].reshape(B, H, S, S)
        key = jax.random.key(seed)
        ks = jax.random.split(key, 8)
        B, S, D, H = (8, 512, 64, NUM_HEADS)
        dh = D // H
        s = 0.02
        return {'inputs': jax.random.normal(ks[0], (B, S, D), dtype=jnp.float32), 'ln_gamma': jnp.ones((D,), jnp.float32), 'ln_beta': jnp.zeros((D,), jnp.float32), 'Wq': jax.random.normal(ks[1], (D, D), jnp.float32) * s, 'bq': jnp.zeros((D,), jnp.float32), 'Wk': jax.random.normal(ks[2], (D, D), jnp.float32) * s, 'bk': jnp.zeros((D,), jnp.float32), 'Wv': jax.random.normal(ks[3], (D, D), jnp.float32) * s, 'bv': jnp.zeros((D,), jnp.float32), 'Wpos': jax.random.normal(ks[4], (D, D), jnp.float32) * s, 'u_bias': jax.random.normal(ks[5], (H, dh), jnp.float32) * s, 'v_bias': jax.random.normal(ks[6], (H, dh), jnp.float32) * s, 'Wout': jax.random.normal(ks[7], (D, D), jnp.float32) * s, 'bout': jnp.zeros((D,), jnp.float32)}
    _L0_attn_all = _L0_attn_setup()
    _L0_attn_in = {k: v for k, v in _L0_attn_all.items() if k in ('ln_gamma', 'ln_beta', 'Wq', 'bq', 'Wk', 'bk', 'Wv', 'bv', 'Wpos', 'u_bias', 'v_bias', 'Wout', 'bout')}
    del _L0_attn_all

    def _L0_ffn_setup():
        import jax, jax.numpy as jnp
        import numpy as np
        B, T, C = (64, 96, 64)
        NH, NKV = (4, 2)
        HD = C // NH
        NREP = NH // NKV
        NE, TOPK = (8, 2)
        HID = int(8 / 3 * C)
        EPS_RMS = 1e-06

        def _rope_tables(t_len):
            inv_freq = 1.0 / 10000.0 ** (np.arange(0, HD, 2, dtype=np.float32) / HD)
            t = np.arange(t_len, dtype=np.float32)
            freqs = np.outer(t, inv_freq)
            emb = np.concatenate([freqs, freqs], axis=-1)
            return (jnp.asarray(np.cos(emb)), jnp.asarray(np.sin(emb)))

        def _rotate_half(x):
            h = x.shape[-1] // 2
            return jnp.concatenate([-x[..., h:], x[..., :h]], axis=-1)

        def _rmsnorm(v, w):
            return v * jax.lax.rsqrt(jnp.mean(v * v, axis=-1, keepdims=True) + EPS_RMS) * w
        key = jax.random.key(seed)
        ks = jax.random.split(key, 10)
        s = lambda k, shape: jax.random.normal(k, shape, jnp.float32) * 0.02
        return {'x': jax.random.normal(ks[0], (B, T, C), jnp.float32), 'ln1_w': jnp.ones((C,), jnp.float32), 'ln2_w': jnp.ones((C,), jnp.float32), 'wq': s(ks[1], (NH * HD, C)), 'wk': s(ks[2], (NKV * HD, C)), 'wv': s(ks[3], (NKV * HD, C)), 'wo': s(ks[4], (C, C)), 'router_w': s(ks[5], (NE, C)), 'w1': s(ks[6], (NE, HID, C)), 'w2': s(ks[7], (NE, C, HID)), 'w3': s(ks[8], (NE, HID, C))}
    _L0_ffn_all = _L0_ffn_setup()
    _L0_ffn_in = {k: v for k, v in _L0_ffn_all.items() if k in ('ln1_w', 'ln2_w', 'wq', 'wk', 'wv', 'wo', 'router_w', 'w1', 'w2', 'w3')}
    del _L0_ffn_all

    def _L1_attn_setup():
        import jax, jax.numpy as jnp
        import numpy as np
        IN_C = 64
        HID_C = 64
        HEADS = 8
        SCALE = 1.0 / np.sqrt(HID_C / HEADS).astype(np.float32)
        key = jax.random.key(seed)
        k_v, k_q, k_k, k_w, k_o, k_b = jax.random.split(key, 6)
        B, S = (4, 512)
        lim_in = 1.0 / np.sqrt(IN_C)
        lim_out = 1.0 / np.sqrt(IN_C * HEADS)
        v = jax.random.normal(k_v, (B, S, IN_C), dtype=jnp.float32)
        WQ = jax.random.uniform(k_q, (IN_C, IN_C * HEADS), jnp.float32, -lim_in, lim_in)
        WK = jax.random.uniform(k_k, (IN_C, IN_C * HEADS), jnp.float32, -lim_in, lim_in)
        WV = jax.random.uniform(k_w, (IN_C, IN_C * HEADS), jnp.float32, -lim_in, lim_in)
        Wout = jax.random.uniform(k_o, (IN_C * HEADS, HID_C), jnp.float32, -lim_out, lim_out)
        bout = jax.random.uniform(k_b, (HID_C,), jnp.float32, -lim_out, lim_out)
        return {'v': v, 'WQ': WQ, 'WK': WK, 'WV': WV, 'Wout': Wout, 'bout': bout}
    _L1_attn_all = _L1_attn_setup()
    _L1_attn_in = {k: v for k, v in _L1_attn_all.items() if k in ('WQ', 'WK', 'WV', 'Wout', 'bout')}
    del _L1_attn_all

    def _L1_ffn_setup():
        import jax, jax.numpy as jnp
        import numpy as np
        E = 8
        K = 2
        D = 64
        H = 128
        DOUT = 64
        EPS = 1e-05
        key = jax.random.key(seed)
        ks = jax.random.split(key, 9)
        s = 0.02
        return {'x': jax.random.normal(ks[0], (4, 2048, D), jnp.float32), 'gamma': 1.0 + 0.05 * jax.random.normal(ks[1], (D,), jnp.float32), 'beta': 0.05 * jax.random.normal(ks[2], (D,), jnp.float32), 'Wr': 0.01 * jax.random.normal(ks[3], (D, E), jnp.float32), 'br': jnp.zeros((E,), jnp.float32), 'W1': s * jax.random.normal(ks[4], (E, D, H), jnp.float32), 'b1': s * jax.random.normal(ks[5], (E, H), jnp.float32), 'W2': s * jax.random.normal(ks[6], (E, H, DOUT), jnp.float32), 'b2': s * jax.random.normal(ks[7], (E, DOUT), jnp.float32)}
    _L1_ffn_all = _L1_ffn_setup()
    _L1_ffn_in = {k: v for k, v in _L1_ffn_all.items() if k in ('gamma', 'beta', 'Wr', 'br', 'W1', 'b1', 'W2', 'b2')}
    del _L1_ffn_all
    return {'x': x, 'L0_tok_token_W': _L0_tok_in['token_W'], 'L0_tok_pe': _L0_tok_in['pe'], 'L0_attn_ln_gamma': _L0_attn_in['ln_gamma'], 'L0_attn_ln_beta': _L0_attn_in['ln_beta'], 'L0_attn_Wq': _L0_attn_in['Wq'], 'L0_attn_bq': _L0_attn_in['bq'], 'L0_attn_Wk': _L0_attn_in['Wk'], 'L0_attn_bk': _L0_attn_in['bk'], 'L0_attn_Wv': _L0_attn_in['Wv'], 'L0_attn_bv': _L0_attn_in['bv'], 'L0_attn_Wpos': _L0_attn_in['Wpos'], 'L0_attn_u_bias': _L0_attn_in['u_bias'], 'L0_attn_v_bias': _L0_attn_in['v_bias'], 'L0_attn_Wout': _L0_attn_in['Wout'], 'L0_attn_bout': _L0_attn_in['bout'], 'L0_ffn_ln1_w': _L0_ffn_in['ln1_w'], 'L0_ffn_ln2_w': _L0_ffn_in['ln2_w'], 'L0_ffn_wq': _L0_ffn_in['wq'], 'L0_ffn_wk': _L0_ffn_in['wk'], 'L0_ffn_wv': _L0_ffn_in['wv'], 'L0_ffn_wo': _L0_ffn_in['wo'], 'L0_ffn_router_w': _L0_ffn_in['router_w'], 'L0_ffn_w1': _L0_ffn_in['w1'], 'L0_ffn_w2': _L0_ffn_in['w2'], 'L0_ffn_w3': _L0_ffn_in['w3'], 'L1_attn_WQ': _L1_attn_in['WQ'], 'L1_attn_WK': _L1_attn_in['WK'], 'L1_attn_WV': _L1_attn_in['WV'], 'L1_attn_Wout': _L1_attn_in['Wout'], 'L1_attn_bout': _L1_attn_in['bout'], 'L1_ffn_gamma': _L1_ffn_in['gamma'], 'L1_ffn_beta': _L1_ffn_in['beta'], 'L1_ffn_Wr': _L1_ffn_in['Wr'], 'L1_ffn_br': _L1_ffn_in['br'], 'L1_ffn_W1': _L1_ffn_in['W1'], 'L1_ffn_b1': _L1_ffn_in['b1'], 'L1_ffn_W2': _L1_ffn_in['W2'], 'L1_ffn_b2': _L1_ffn_in['b2']}

def reference(x, L0_tok_token_W, L0_tok_pe, L0_attn_ln_gamma, L0_attn_ln_beta, L0_attn_Wq, L0_attn_bq, L0_attn_Wk, L0_attn_bk, L0_attn_Wv, L0_attn_bv, L0_attn_Wpos, L0_attn_u_bias, L0_attn_v_bias, L0_attn_Wout, L0_attn_bout, L0_ffn_ln1_w, L0_ffn_ln2_w, L0_ffn_wq, L0_ffn_wk, L0_ffn_wv, L0_ffn_wo, L0_ffn_router_w, L0_ffn_w1, L0_ffn_w2, L0_ffn_w3, L1_attn_WQ, L1_attn_WK, L1_attn_WV, L1_attn_Wout, L1_attn_bout, L1_ffn_gamma, L1_ffn_beta, L1_ffn_Wr, L1_ffn_br, L1_ffn_W1, L1_ffn_b1, L1_ffn_W2, L1_ffn_b2):
    import jax
    import jax.numpy as jnp

    def _L0_tok_ref(sequence, token_W, pe):
        import jax, jax.numpy as jnp
        import numpy as np
        VOCAB = 128
        D = 64
        S = 128
        B = 128
        MAX_LEN = 128
        SEP_ID = 13
        PAD_ID = 1

        def _make_pe():
            pos = np.arange(MAX_LEN, dtype=np.float32)[:, None]
            div = np.exp(np.arange(0, D, 2, dtype=np.float32) * (-np.log(10000.0) / D))
            pe = np.zeros((MAX_LEN, D), dtype=np.float32)
            pe[:, 0::2] = np.sin(pos * div)
            pe[:, 1::2] = np.cos(pos * div)
            return jnp.asarray(pe)
        tok_emb = token_W[sequence] * (sequence != 0)[..., None].astype(token_W.dtype)
        S_, B_ = sequence.shape

        def step(carry, xs):
            prev_sep, pad_num = carry
            tok, j = xs
            is_sep = tok == SEP_ID
            skip = prev_sep & (tok == PAD_ID) & ~is_sep
            pos_emb = pe[j - pad_num]
            emb = jnp.where(skip[:, None], jnp.zeros((), pe.dtype), pos_emb)
            new_carry = (is_sep | skip, pad_num + skip.astype(pad_num.dtype))
            return (new_carry, emb)
        init = (jnp.zeros((B_,), dtype=bool), jnp.zeros((B_,), dtype=jnp.int32))
        _, pos_emb = jax.lax.scan(step, init, (sequence, jnp.arange(S_, dtype=jnp.int32)))
        return tok_emb + pos_emb

    def _L0_attn_ref(inputs, ln_gamma, ln_beta, Wq, bq, Wk, bk, Wv, bv, Wpos, u_bias, v_bias, Wout, bout):
        import jax, jax.numpy as jnp
        import numpy as np
        NUM_HEADS = 4
        LN_EPS = 1e-05

        def positional_encoding(length, d_model):
            pos = jnp.arange(length, dtype=jnp.float32)[:, None]
            div = jnp.exp(jnp.arange(0, d_model, 2, dtype=jnp.float32) * (-np.log(10000.0) / d_model))
            pe = jnp.zeros((length, d_model), dtype=jnp.float32)
            pe = pe.at[:, 0::2].set(jnp.sin(pos * div))
            pe = pe.at[:, 1::2].set(jnp.cos(pos * div))
            return pe

        def rel_shift(pos_score):
            B, H, S, _ = pos_score.shape
            padded = jnp.pad(pos_score, ((0, 0), (0, 0), (0, 0), (1, 0)))
            padded = padded.reshape(B, H, S + 1, S)
            return padded[:, :, 1:].reshape(B, H, S, S)
        B, S, D = inputs.shape
        H = NUM_HEADS
        dh = D // H
        mu = jnp.mean(inputs, axis=-1, keepdims=True)
        var = jnp.mean(jnp.square(inputs - mu), axis=-1, keepdims=True)
        x = (inputs - mu) / jnp.sqrt(var + LN_EPS) * ln_gamma + ln_beta
        pe = positional_encoding(S, D)
        q = (x @ Wq + bq).reshape(B, S, H, dh)
        k = (x @ Wk + bk).reshape(B, S, H, dh)
        v = (x @ Wv + bv).reshape(B, S, H, dh)
        p = (pe @ Wpos).reshape(S, H, dh)
        content_score = jnp.einsum('bshd,bthd->bhst', q + u_bias, k)
        pos_score = jnp.einsum('bshd,thd->bhst', q + v_bias, p)
        pos_score = rel_shift(pos_score)
        score = (content_score + pos_score) / np.sqrt(D).astype(np.float32)
        attn = jax.nn.softmax(score, axis=-1)
        ctx = jnp.einsum('bhst,bthd->bshd', attn, v).reshape(B, S, D)
        return ctx @ Wout + bout

    def _L0_ffn_ref(x, ln1_w, ln2_w, wq, wk, wv, wo, router_w, w1, w2, w3):
        import jax, jax.numpy as jnp
        import numpy as np
        B, T, C = (64, 96, 64)
        NH, NKV = (4, 2)
        HD = C // NH
        NREP = NH // NKV
        NE, TOPK = (8, 2)
        HID = int(8 / 3 * C)
        EPS_RMS = 1e-06

        def _rope_tables(t_len):
            inv_freq = 1.0 / 10000.0 ** (np.arange(0, HD, 2, dtype=np.float32) / HD)
            t = np.arange(t_len, dtype=np.float32)
            freqs = np.outer(t, inv_freq)
            emb = np.concatenate([freqs, freqs], axis=-1)
            return (jnp.asarray(np.cos(emb)), jnp.asarray(np.sin(emb)))

        def _rotate_half(x):
            h = x.shape[-1] // 2
            return jnp.concatenate([-x[..., h:], x[..., :h]], axis=-1)

        def _rmsnorm(v, w):
            return v * jax.lax.rsqrt(jnp.mean(v * v, axis=-1, keepdims=True) + EPS_RMS) * w
        Bx, Tx, Cx = x.shape
        h = _rmsnorm(x, ln1_w)
        q = (h @ wq.T).reshape(Bx, Tx, NH, HD).transpose(0, 2, 1, 3)
        k = (h @ wk.T).reshape(Bx, Tx, NKV, HD).transpose(0, 2, 1, 3)
        v = (h @ wv.T).reshape(Bx, Tx, NKV, HD).transpose(0, 2, 1, 3)
        cos, sin = _rope_tables(Tx)
        cos, sin = (cos[None, None], sin[None, None])
        q = q * cos + _rotate_half(q) * sin
        k = k * cos + _rotate_half(k) * sin
        k = jnp.repeat(k, NREP, axis=1)
        v = jnp.repeat(v, NREP, axis=1)
        scores = jnp.einsum('bhtd,bhsd->bhts', q, k) / jnp.sqrt(jnp.float32(HD))
        causal = jnp.tril(jnp.ones((Tx, Tx), dtype=bool))
        scores = jnp.where(causal[None, None], scores, jnp.float32(-1e+30))
        att = jax.nn.softmax(scores, axis=-1)
        y = jnp.einsum('bhts,bhsd->bhtd', att, v).transpose(0, 2, 1, 3).reshape(Bx, Tx, Cx)
        x = x + y @ wo.T
        flat = _rmsnorm(x, ln2_w).reshape(-1, Cx)
        probs = jax.nn.softmax(flat @ router_w.T, axis=-1)
        tp, ti = jax.lax.top_k(probs, TOPK)
        tp = tp / (jnp.sum(tp, axis=-1, keepdims=True) + 1e-09)
        weights = jnp.sum(tp[..., None] * jax.nn.one_hot(ti, NE, dtype=flat.dtype), axis=1)
        out = jnp.zeros_like(flat)
        for e in range(NE):
            hh = jax.nn.silu(flat @ w1[e].T) * (flat @ w3[e].T)
            out = out + weights[:, e:e + 1] * (hh @ w2[e].T)
        return x + out.reshape(Bx, Tx, Cx)

    def _L1_attn_ref(v, WQ, WK, WV, Wout, bout):
        import jax, jax.numpy as jnp
        import numpy as np
        IN_C = 64
        HID_C = 64
        HEADS = 8
        SCALE = 1.0 / np.sqrt(HID_C / HEADS).astype(np.float32)
        B, S, C = v.shape
        H = HEADS
        q = (v @ WQ).reshape(B, S, H, C)
        k = (v @ WK).reshape(B, S, H, C)
        val = (v @ WV).reshape(B, S, H, C)
        scores = jnp.einsum('bshc,bthc->bsth', q, k) * SCALE
        A = jax.nn.softmax(scores, axis=2)
        u = jnp.einsum('bsth,bthc->bshc', A, val).reshape(B, S, H * C)
        return u @ Wout + bout

    def _L1_ffn_ref(x, gamma, beta, Wr, br, W1, b1, W2, b2):
        import jax, jax.numpy as jnp
        import numpy as np
        E = 8
        K = 2
        D = 64
        H = 128
        DOUT = 64
        EPS = 1e-05
        mu = jnp.mean(x, axis=-1, keepdims=True)
        var = jnp.mean(jnp.square(x - mu), axis=-1, keepdims=True)
        xn = (x - mu) * jax.lax.rsqrt(var + EPS) * gamma + beta
        logits = jnp.einsum('bsd,de->bse', xn, Wr) + br
        top_vals, top_idx = jax.lax.top_k(logits, K)
        w = jax.nn.softmax(top_vals, axis=-1)
        w_full = jnp.einsum('bsk,bske->bse', w, jax.nn.one_hot(top_idx, E, dtype=w.dtype))
        y = jnp.zeros(x.shape[:-1] + (DOUT,), x.dtype)
        for e in range(E):
            h = jax.nn.gelu(jnp.einsum('bsd,dh->bsh', xn, W1[e]) + b1[e], approximate=False)
            y_e = jnp.einsum('bsh,hd->bsd', h, W2[e]) + b2[e]
            y = y + y_e * w_full[..., e, None]
        return y
    h = _L0_tok_ref(x, L0_tok_token_W, L0_tok_pe)
    h = h + _L0_attn_ref(_layernorm(h, axis=-1), L0_attn_ln_gamma, L0_attn_ln_beta, L0_attn_Wq, L0_attn_bq, L0_attn_Wk, L0_attn_bk, L0_attn_Wv, L0_attn_bv, L0_attn_Wpos, L0_attn_u_bias, L0_attn_v_bias, L0_attn_Wout, L0_attn_bout)
    h = h + _L0_ffn_ref(_layernorm(h, axis=-1), L0_ffn_ln1_w, L0_ffn_ln2_w, L0_ffn_wq, L0_ffn_wk, L0_ffn_wv, L0_ffn_wo, L0_ffn_router_w, L0_ffn_w1, L0_ffn_w2, L0_ffn_w3)
    h = h + _L1_attn_ref(_layernorm(h, axis=-1), L1_attn_WQ, L1_attn_WK, L1_attn_WV, L1_attn_Wout, L1_attn_bout)
    h = h + _L1_ffn_ref(_layernorm(h, axis=-1), L1_ffn_gamma, L1_ffn_beta, L1_ffn_Wr, L1_ffn_br, L1_ffn_W1, L1_ffn_b1, L1_ffn_W2, L1_ffn_b2)
    return h

_drawn_inputs = setup_inputs


def setup_inputs(seed=0):
    import zlib

    import numpy as np

    out = dict(_drawn_inputs(seed))
    spreads = {'L0_attn_ln_gamma': (1.0, 0.6),
     'L0_attn_ln_beta': (0.0, 0.8),
     'L0_attn_bq': (0.0, 2.0),
     'L0_attn_bk': (0.0, 2.0),
     'L0_attn_bv': (0.0, 0.1),
     'L0_attn_bout': (0.0, 0.1),
     'L0_ffn_ln1_w': (1.0, 0.6),
     'L0_ffn_ln2_w': (1.0, 0.6),
     'L1_ffn_br': (0.0, 0.566)}
    factors = {'L0_attn_Wq': 64.0,
     'L0_attn_Wk': 64.0,
     'L0_attn_Wpos': 64.0,
     'L0_attn_u_bias': 194.756,
     'L0_attn_v_bias': 64.0,
     'L0_ffn_wq': 8.0,
     'L0_ffn_wk': 27.085,
     'L0_ffn_wv': 3.117,
     'L0_ffn_router_w': 8.0,
     'L0_ffn_w1': 8.0,
     'L0_ffn_w2': 8.0,
     'L0_ffn_w3': 8.0,
     'L1_attn_WQ': 8.0,
     'L1_attn_WK': 8.0,
     'L1_attn_bout': 3.131,
     'L1_ffn_gamma': 8.0,
     'L1_ffn_beta': 8.0,
     'L1_ffn_Wr': 4.812,
     'L1_ffn_W1': 6.242,
     'L1_ffn_b1': 27.729,
     'L1_ffn_W2': 6.384,
     'L1_ffn_b2': 33.3}
    for name, (base, spread) in spreads.items():
        noise = np.random.default_rng([zlib.crc32(name.encode()), seed]).standard_normal(out[name].shape)
        drawn = base * np.exp(spread * noise) if base else spread * noise
        out[name] = jnp.asarray(drawn.astype(out[name].dtype))
    for name, factor in factors.items():
        out[name] = (out[name] * factor).astype(out[name].dtype)
    return out
```

```python
import numpy as np
import concourse.bass as bass
from concourse import mybir
from contextlib import ExitStack

F32 = mybir.dt.float32
F32R = mybir.dt.float32r
I32 = mybir.dt.int32
ALU = mybir.AluOpType
ACT = mybir.ActivationFunctionType
AX = mybir.AxisListType

P = 128
B, S, D = 2, 2048, 64
N = B * S
NT = N // P
TPB = S // P
BANK = 512
VOCAB = 128
SEP_ID, PAD_ID = 13, 1
E = 8
LN_EPS, RMS_EPS = 1e-5, 1e-6
NEG = -1e30


class Machine:

    def __init__(self, nc, whole):
        self.nc, self.whole, self.stage_no, self.sems = nc, whole, 0, []

    def sbuf(self, name, shape, dtype=F32, ctx=None):
        return (ctx or self.whole).enter_context(self.nc.sbuf_tensor(name, shape, dtype))

    def sem(self, name):
        self.sems.append(self.nc.alloc_semaphore(name=name))
        return self.sems[-1]

    def renew_semaphores(self):
        self.nc.clear_and_free_semaphores(self.sems)
        self.nc.all_engine_barrier()
        self.sems = []

    def stage(self, name):
        self.stage_no += 1
        return f"{name}{self.stage_no}"


def bcast(ap, shape, axis):
    return ap.unsqueeze(axis).broadcast_to(shape)


def tiles(t, k=NT):
    return t[:].rearrange("p (t c) -> p t c", t=k)


def embed(m, tokens, token_W, pe_rows, iota):
    nc, tag = m.nc, m.stage("embed")
    with ExitStack() as c:
        ids = m.sbuf("ids", [P, N], I32, c)
        onehot = m.sbuf("onehot", [P, N], F32, c)
        table = m.sbuf("table", [VOCAB, D], F32, c)
        col = m.sbuf("iota_col", [P, 1], F32, c)
        pe01 = m.sbuf("pe01", [1, 2 * D], F32, c)
        is_sep = m.sbuf("is_sep", [1, S], F32, c)
        is_pad = m.sbuf("is_pad", [1, S], F32, c)
        posed = m.sbuf("posed", [1, N], F32, c)
        loaded, hot, mask_step = m.sem(tag + "_loaded"), m.sem(tag + "_hot"), m.sem(tag + "_mask")
        summed, kept = m.sem(tag + "_summed"), m.sem(tag + "_kept")
        block = c.enter_context(nc.Block())
        PER = BANK // D

        @block.sync
        def _(sp):
            sp.dma_start(ids[:], tokens.rearrange("s b -> (s b)").partition_broadcast(P)).then_inc(loaded, 16)
            sp.dma_start(table[:], token_W).then_inc(loaded, 16)
            sp.dma_start(col[:], iota).then_inc(loaded, 16)
            sp.dma_start(pe01[:], pe_rows).then_inc(loaded, 16)

        @block.vector
        def _(dve):
            dve.wait_ge(loaded, 64)
            nc.vector.tensor_scalar(onehot[:], ids[:], col[:, 0:1], None, ALU.is_equal).then_inc(hot, 1)
            nc.vector.memset(posed[0:1, 0:S], 1.0).then_inc(mask_step, 1)
            nc.vector.tensor_scalar(is_sep[:], ids[0:1, 0:S], float(SEP_ID), None, ALU.is_equal).then_inc(mask_step, 1)
            nc.vector.tensor_scalar(is_pad[:], ids[0:1, S:N], float(PAD_ID), None, ALU.is_equal).then_inc(mask_step, 1)
            dve.wait_ge(mask_step, 3)
            nc.vector.tensor_tensor(is_sep[:], is_sep[:], is_pad[:], ALU.mult).then_inc(mask_step, 1)
            dve.wait_ge(mask_step, 4)
            nc.vector.tensor_scalar(posed[0:1, S:N], is_sep[:], -1.0, 1.0, ALU.mult, ALU.add).then_inc(mask_step, 1)
            for g in range(NT // PER):
                dve.wait_ge(summed, g + 1)
                nc.vector.tensor_copy(m.H[:, g * BANK:(g + 1) * BANK], m.bank(g % 2)).then_inc(kept, 1)

        @block.tensor
        def _(pe):
            pe.wait_ge(hot, 1)
            pe.wait_ge(mask_step, 5)
            for t in range(NT):
                g, j = t // PER, t % PER
                if j == 0 and g >= 2:
                    pe.wait_ge(kept, g - 1)
                out = m.bank(g % 2)[:, j * D:(j + 1) * D]
                nc.tensor.matmul(out, onehot[:, t * P:(t + 1) * P], table[:], start=True, stop=False)
                s = t // TPB
                last = nc.tensor.matmul(out, posed[0:1, t * P:(t + 1) * P], pe01[0:1, s * D:(s + 1) * D],
                                        start=False, stop=True)
                if j == PER - 1:
                    last.then_inc(summed, 1)


def normalize(m, src, dst, eps, mean=True, gamma=None, beta=None):
    nc, tag = m.nc, m.stage("norm")
    with ExitStack() as c:
        square = m.sbuf(tag + "_square", [P, NT * D], F32, c)
        stat = m.sbuf(tag + "_stat", [P, 4 * NT], F32, c)
        affine = m.sbuf(tag + "_affine", [P, 2 * D], F32, c)
        eps_col = m.sbuf(tag + "_eps", [P, 1], F32, c)
        sums, means, var, rstd = (stat[:, k * NT:(k + 1) * NT] for k in range(4))
        step, loaded = m.sem(tag + "_step"), m.sem(tag + "_loaded")
        squared, rooted = m.sem(tag + "_squared"), m.sem(tag + "_rooted")
        block = c.enter_context(nc.Block())
        shape = [P, NT, D]
        loads = [(k, v) for k, v in enumerate((gamma, beta)) if v is not None]

        @block.sync
        def _(sp):
            for k, v in loads:
                sp.dma_start(affine[:, k * D:(k + 1) * D], v.partition_broadcast(P)).then_inc(loaded, 16)

        @block.gpsimd
        def _(pool):
            pool.wait_ge(step, 3 if mean else 1)
            nc.gpsimd.tensor_tensor(square[:], dst[:] if mean else src[:], dst[:] if mean else src[:],
                                    ALU.mult).then_inc(squared, 1)

        @block.scalar
        def _(act):
            act.wait_ge(step, 4 if mean else 2)
            nc.scalar.activation(var, var, ACT.Sqrt, bias=eps_col[:, 0:1], scale=1.0 / D).then_inc(rooted, 1)

        @block.vector
        def _(dve):
            n = 0

            def done(instruction):
                nonlocal n
                n += 1
                instruction.then_inc(step, 1)
                dve.wait_ge(step, n)

            if mean:
                done(nc.vector.tensor_reduce(sums, tiles(src), axis=AX.X, op=ALU.add))
                done(nc.vector.tensor_scalar(means, sums, 1.0 / D, None, ALU.mult))
                nc.vector.memset(eps_col[:], eps)
                done(nc.vector.tensor_tensor(tiles(dst), tiles(src), bcast(means, shape, 2), ALU.subtract))
            else:
                done(nc.vector.memset(eps_col[:], eps))
            dve.wait_ge(squared, 1)
            done(nc.vector.tensor_reduce(var, tiles(square), axis=AX.X, op=ALU.add))
            dve.wait_ge(rooted, 1)
            done(nc.vector.reciprocal(rstd, var))
            done(nc.vector.tensor_tensor(tiles(dst), tiles(dst if mean else src), bcast(rstd, shape, 2), ALU.mult))
            if loads:
                dve.wait_ge(loaded, 16 * len(loads))
            for k, _ in loads:
                done(nc.vector.tensor_tensor(tiles(dst), tiles(dst), bcast(affine[:, k * D:(k + 1) * D], shape, 1),
                                             ALU.mult if k == 0 else ALU.add))


def channels_first(m, src, dst, blocks=1, ones=0):
    nc, tag = m.nc, m.stage("turn")
    turned, copied_v, copied_s = m.sem(tag + "_turned"), m.sem(tag + "_copied_v"), m.sem(tag + "_copied_s")
    PER = BANK // P
    groups = NT // PER
    with ExitStack() as c:
        block = c.enter_context(nc.Block())

        @block.tensor
        def _(pe):
            for g in range(groups):
                if g >= 4:
                    pe.wait_ge(copied_s if g % 2 else copied_v, (g - 4) // 2 + 1)
                for j in range(PER):
                    t = g * PER + j
                    last = nc.tensor.transpose(m.bank(g % 4)[0:D, j * P:(j + 1) * P],
                                               src[:, t * D:(t + 1) * D], m.ident[:])
                last.then_inc(turned, 1)

        @block.vector
        def _(dve):
            for g in range(0, groups, 2):
                dve.wait_ge(turned, g + 1)
                nc.vector.tensor_copy(dst[0:D, g * BANK:(g + 1) * BANK], m.bank(g % 4)[0:D, :]).then_inc(copied_v, 1)

        @block.scalar
        def _(act):
            for g in range(1, groups, 2):
                act.wait_ge(turned, g + 1)
                nc.scalar.activation(dst[0:D, g * BANK:(g + 1) * BANK], m.bank(g % 4)[0:D, :],
                                     ACT.Copy).then_inc(copied_s, 1)

        if ones:
            @block.gpsimd
            def _(pool):
                nc.gpsimd.memset(dst[D:D + ones, :], 1.0)


def project_add(m, ctxT, rows, weight, dst):
    nc, tag = m.nc, m.stage("out")
    PER = BANK // D
    with ExitStack() as c:
        w = m.sbuf(tag + "_w", [rows, D], F32, c)
        loaded, made, added = m.sem(tag + "_loaded"), m.sem(tag + "_made"), m.sem(tag + "_added")
        block = c.enter_context(nc.Block())

        @block.sync
        def _(sp):
            sp.dma_start(w[:], weight).then_inc(loaded, 16)

        @block.tensor
        def _(pe):
            pe.wait_ge(loaded, 16)
            for t in range(NT):
                g, j = t // PER, t % PER
                if j == 0 and g >= 2:
                    pe.wait_ge(added, g - 1)
                last = nc.tensor.matmul(m.bank(g % 2)[:, j * D:(j + 1) * D], ctxT[0:rows, t * P:(t + 1) * P],
                                        w[:], start=True, stop=True)
                if j == PER - 1:
                    last.then_inc(made, 1)

        @block.vector
        def _(dve):
            for g in range(NT // PER):
                dve.wait_ge(made, g + 1)
                nc.vector.tensor_tensor(dst[:, g * BANK:(g + 1) * BANK], m.bank(g % 2),
                                        dst[:, g * BANK:(g + 1) * BANK], ALU.add).then_inc(added, 1)


class HeadPlan:

    def __init__(self, causal, width):
        self.causal = causal
        self.width = width
        self.groups = P // width
        self.keys = [(i + 1) * P if causal else S for i in range(TPB)]
        self.banks = [-(-k // BANK) for k in self.keys]
        self.bank_sum = self.before(self.banks)
        self.halves = [-(-b // 2) for b in self.banks]
        self.half_sum = self.before(self.halves)
        self.copier = [["s" if (g != 3 and b > 1) or (b == 1 and i % 2) else "v" for g in range(b)]
                       for i, b in enumerate(self.banks)]
        self.copies = {w: self.before([row.count(w) for row in self.copier]) for w in "sv"}

    @staticmethod
    def before(counts):
        out = [0]
        for c in counts:
            out.append(out[-1] + c)
        return out

    def cols(self, i, k):
        return k * BANK, min((k + 1) * BANK, self.keys[i])

    def copied(self, i, g):
        w = self.copier[i][g]
        return w, self.copies[w][i] + self.copier[i][:g + 1].count(w)

    def of_use(self, u):
        i = max(n for n in range(TPB) if self.bank_sum[n] <= u)
        return i, u - self.bank_sum[i]


def attention(m, kind, heads, ctx_cols, prepare, spare=None):
    nc, tag = m.nc, m.stage(kind)
    causal, rel, wide = kind == "causal", kind == "relative", kind == "wide"
    plan = HeadPlan(causal, 64 if wide else 32)
    dh = ctx_cols
    W = plan.width
    with ExitStack() as c:
        probs = [spare or m.sbuf(f"{tag}_probs0", [P, S], F32, c), m.sbuf(f"{tag}_probs1", [P, S], F32, c)]
        probsT = [m.sbuf(f"{tag}_probsT{k}", [P, S], F32, c) for k in range(2)]
        outT = [m.sbuf(f"{tag}_outT{k}", [P, P], F32, c) for k in range(2)]
        stat = m.sbuf(tag + "_stat", [P, 4 * 16], F32, c)
        values = m.sbuf(tag + "_values", [P, TPB * W], F32, c)
        names = ("score_ready diag_ready fixed max_step bias_ready exp_done turned copied_s copied_v out_ready "
                 "outT_done joined normed values_in norm_step sum_step").split()
        sems = {n: m.sem(f"{tag}_{n}") for n in names}
        (score_ready, diag_ready, fixed, max_step, bias_ready, exp_done, turned, copied_s, copied_v, out_ready,
         outT_done, joined, normed, values_in, norm_step, sum_step) = (sems[n] for n in names)
        copied = {"s": copied_s, "v": copied_v}
        block = c.enter_context(nc.Block())
        T_BANK, O_BANK, M_BANK = 4, 6, 7
        ops = prepare(m, tag, c, normed)
        scores = m.psum

        def bias_cols(i):
            k = (i % 4) * 16
            return stat[:, k:k + 4], stat[:, k + 4:k + 5], stat[:, k + 5:k + 7], stat[:, k + 7:k + 8], \
                stat[:, k + 8:k + 9]
        HB, HH = plan.bank_sum[TPB], plan.half_sum[TPB]
        HC = {w: plan.copies[w][TPB] for w in "sv"}

        def exp_covers(i, k):
            return plan.half_sum[i] + k // 2 + 1

        @block.sync
        def _(sp):
            ops.load_weights(sp, 0)
            sp.dma_start(values[:], ops.values_of(0)).then_inc(values_in, 16)
            with sp.Fori(1, B * heads) as it:
                sp.wait_ge(ops.weights_used, it * ops.uses)
                ops.load_weights(sp, it)
                sp.wait_ge(normed, it * TPB)
                sp.dma_start(values[:], ops.values_of(it)).then_inc(values_in, 16)

        @block.tensor
        def _(pe):
            with pe.Fori(0, B) as b, pe.Fori(0, heads) as h:
                it = b * heads + h
                ops.pe_prepare(pe, it, b)
                for step in range(TPB + 2):
                    i = step
                    if i < TPB:
                        if rel:
                            if i >= 3:
                                pe.wait_ge(normed, it * TPB + i - 2)
                            if i >= 1:
                                pe.wait_ge(fixed, (it * TPB + i) * 2)
                            ops.diagonal(i, m.bank(M_BANK)).then_inc(diag_ready, 1)
                        for k in range(plan.banks[i]):
                            if i and k < plan.banks[i - 1] and k % 2 == 0:
                                pe.wait_ge(exp_done, it * HH + exp_covers(i - 1, k))
                            ops.scores(i, *plan.cols(i, k)).then_inc(score_ready, 1)
                    j = step - 1
                    if 0 <= j < TPB:
                        if j == 0:
                            pe.wait_ge(values_in, 16 * (it + 1))
                        for g in range(plan.banks[j] + 1):
                            if g < plan.banks[j]:
                                pe.wait_ge(exp_done, it * HH + exp_covers(j, g))
                                u = plan.bank_sum[j] + g
                                if u >= 2:
                                    w, n = plan.copied(*plan.of_use(u - 2))
                                    pe.wait_ge(copied[w], it * HC[w] + n)
                                lo, hi = plan.cols(j, g)
                                for q in range((hi - lo) // P):
                                    last = nc.tensor.transpose(m.bank(T_BANK + u % 2)[:, q * P:(q + 1) * P],
                                                               probs[j % 2][:, lo + q * P:lo + (q + 1) * P], m.ident[:])
                                last.then_inc(turned, 1)
                            if g >= 1:
                                w, n = plan.copied(j, g - 1)
                                pe.wait_ge(copied[w], it * HC[w] + n)
                                if g == 1 and j >= 1:
                                    pe.wait_ge(outT_done, it * TPB + j)
                                lo, hi = plan.cols(j, g - 1)
                                for kt in range(lo // P, hi // P):
                                    q = kt % plan.groups
                                    last = nc.tensor.matmul(
                                        m.bank(O_BANK)[q * W:(q + 1) * W, 0:P], values[:, kt * W:(kt + 1) * W],
                                        probsT[j % 2][:, kt * P:(kt + 1) * P], start=kt < plan.groups,
                                        stop=kt >= plan.keys[j] // P - plan.groups, skip_group_check=True)
                        last.then_inc(out_ready, 1)
                    j = step - 2
                    if 0 <= j < TPB:
                        rows = min(plan.keys[j] // P, plan.groups) * W
                        pe.wait_ge(outT_done, it * TPB + j + 1)
                        if j >= 1:
                            pe.wait_ge(normed, it * TPB + j)
                        if rel and step < TPB:
                            pe.wait_ge(fixed, (it * TPB + step) * 2 + 2)
                        nc.tensor.matmul(m.bank(M_BANK)[:, 0:W], outT[j % 2][0:rows, :],
                                         m.join[W][0:rows, :], start=True, stop=True).then_inc(joined, 1)
                pe.wait_ge(normed, (it + 1) * TPB)

        @block.scalar
        def _(act):
            with act.Fori(0, B) as b, act.Fori(0, heads) as h:
                it = b * heads + h
                ops.act_prepare(act, it)
                for step in range(TPB + 1):
                    j = step - 1
                    if j >= 0:
                        for g in range(plan.banks[j]):
                            if plan.copier[j][g] == "s":
                                act.wait_ge(turned, it * HB + plan.bank_sum[j] + g + 1)
                                lo, hi = plan.cols(j, g)
                                u = plan.bank_sum[j] + g
                                nc.scalar.activation(probsT[j % 2][:, lo:hi], m.bank(T_BANK + u % 2)[:, 0:hi - lo],
                                                     ACT.Copy).then_inc(copied_s, 1)
                    i = step
                    if i < TPB:
                        act.wait_ge(bias_ready, it * TPB + i + 1)
                        for half in range(plan.halves[i]):
                            lo, hi = 2 * half * BANK, min(2 * (half + 1) * BANK, plan.keys[i])
                            nc.scalar.activation(probs[i % 2][:, lo:hi], scores[:, lo:hi], ACT.Exp,
                                                 bias=bias_cols(i)[1], scale=1.0,
                                                 accum_out=bias_cols(i)[2][:, half:half + 1] if wide else None
                                                 ).then_inc(exp_done, 1)
                    if j >= 0:
                        rows = min(plan.keys[j] // P, plan.groups) * W
                        act.wait_ge(out_ready, it * TPB + j + 1)
                        nc.scalar.activation(outT[j % 2][0:rows, :], m.bank(O_BANK)[0:rows, 0:P],
                                             ACT.Copy).then_inc(outT_done, 1)

        @block.vector
        def _(dve):
            with dve.Fori(0, B) as b, dve.Fori(0, heads) as h:
                it = b * heads + h
                ops.dve_prepare(dve, it)
                for step in range(TPB + 2):
                    i = step
                    if i < TPB:
                        part, bias = bias_cols(i)[:2]
                        diag = (i * P) // BANK
                        seen = -1

                        def wait_bank(k):
                            dve.wait_ge(score_ready, it * HB + plan.bank_sum[i] + k + 1)

                        for k in range(plan.banks[i]):
                            wait_bank(k)
                            if k == diag and rel:
                                if (i + 1) * P == (k + 1) * BANK and i < TPB - 1:
                                    wait_bank(k + 1)
                                dve.wait_ge(diag_ready, it * TPB + i + 1)
                                for n, (lo, hi, mask, data) in enumerate(ops.fixes(i, m.bank(M_BANK))):
                                    nc.vector.memset(stat[:, 15:16], 0.0)
                                    nc.vector.copy_predicated(scores[:, lo:hi], mask, data).then_inc(fixed, 1)
                                    dve.wait_ge(fixed, (it * TPB + i) * 2 + n + 1)
                            if k == diag and causal:
                                nc.vector.tensor_tensor(scores[:, i * P:(i + 1) * P], scores[:, i * P:(i + 1) * P],
                                                        m.causal_mask[:], ALU.add).then_inc(fixed, 1)
                                dve.wait_ge(fixed, it * TPB + i + 1)
                            lo, hi = plan.cols(i, k)
                            last = nc.vector.tensor_reduce(part[:, k:k + 1], scores[:, lo:hi], axis=AX.X, op=ALU.max)
                            last.then_inc(max_step, 1)
                        dve.wait_ge(max_step, it * HB + plan.bank_sum[i] + plan.banks[i])
                        nc.vector.tensor_reduce(bias, part[:, 0:plan.banks[i]], axis=AX.X, op=ALU.max,
                                                negate=True).then_inc(bias_ready, 1)
                    j = step - 1
                    if 0 <= j < TPB:
                        for g in range(plan.banks[j]):
                            if plan.copier[j][g] == "v":
                                dve.wait_ge(turned, it * HB + plan.bank_sum[j] + g + 1)
                                lo, hi = plan.cols(j, g)
                                u = plan.bank_sum[j] + g
                                nc.vector.tensor_copy(probsT[j % 2][:, lo:hi],
                                                      m.bank(T_BANK + u % 2)[:, 0:hi - lo]).then_inc(copied_v, 1)
                    j = step - 2
                    if j >= 0:
                        sums, total, recip = bias_cols(j)[2:]
                        made = m.bank(M_BANK)
                        dve.wait_ge(joined, it * TPB + j + 1)
                        if wide:
                            nc.vector.tensor_reduce(total, sums, axis=AX.X, op=ALU.add).then_inc(sum_step, 1)
                            dve.wait_ge(sum_step, it * TPB + j + 1)
                        nc.vector.reciprocal(recip, total if wide else made[:, dh:dh + 1]).then_inc(norm_step, 1)
                        dve.wait_ge(norm_step, it * TPB + j + 1)
                        nc.vector.tensor_scalar(ops.context(b, h, j), made[:, 0:dh], recip, None,
                                                ALU.mult).then_inc(normed, 1)

        @block.gpsimd
        def _(pool):
            with pool.Fori(0, B) as b, pool.Fori(0, heads) as h:
                it = b * heads + h
                ops.pool_prepare(pool, it)


class Operands:
    pass


def split_columns():
    row = np.arange(P)
    lo_q, lo_k, lo_w = (row // 32) % 2, (row // 16) % 2, row // 64
    cols = [lo_q / 8, 1 - 2 * lo_q, lo_k, 1 - 2 * lo_k, lo_w, 1 - 2 * lo_w, lo_q / 4, 0 * row + 1]
    return np.stack(cols, 1).astype(np.float32)


def all_values(m, XT, rows, weight, kind, Vall):
    nc, tag = m.nc, m.stage("values")
    wide = kind == "wide"
    cols = weight.shape[1]
    W, heads = (64, 8) if wide else (32, 4)
    per = BANK // cols
    V = Vall[:].rearrange("p (b h t w) -> p b h t w", b=B, h=heads, t=TPB)
    with ExitStack() as c:
        w = m.sbuf(tag + "_w", [rows, cols], F32, c)
        loaded, made, kept, cleared = (m.sem(tag + x) for x in ("_loaded", "_made", "_kept", "_cleared"))
        block = c.enter_context(nc.Block())

        @block.sync
        def _(sp):
            sp.dma_start(w[:], weight).then_inc(loaded, 16)

        @block.gpsimd
        def _(pool):
            if not wide:
                nc.gpsimd.memset(Vall[:], 0.0).then_inc(cleared, 1)
                pool.wait_ge(cleared, 1)
                nc.gpsimd.memset(Vall[:].rearrange("p (n w) -> p n w", w=W)[:, :, 16:17], 1.0).then_inc(cleared, 1)

        @block.tensor
        def _(pe):
            pe.wait_ge(loaded, 16)
            for t in range(NT):
                g, j = t // per, t % per
                if j == 0 and g >= 2:
                    pe.wait_ge(kept, g - 1)
                last = nc.tensor.matmul(m.bank(g % 2)[:, j * cols:(j + 1) * cols], XT[0:rows, t * P:(t + 1) * P],
                                        w[:], start=True, stop=True)
                if j == per - 1:
                    last.then_inc(made, 1)

        @block.vector
        def _(dve):
            if not wide:
                dve.wait_ge(cleared, 2)
            for g in range(NT // per):
                dve.wait_ge(made, g + 1)
                b, t = g * per // TPB, g * per % TPB
                if wide:
                    nc.vector.tensor_copy(V[:, b, :, t, :],
                                          m.bank(g % 2).rearrange("p (h d) -> p h d", h=heads)).then_inc(kept, 1)
                    continue
                kv = cols // 16
                for j in range(per):
                    made_kv = m.bank(g % 2)[:, j * cols:(j + 1) * cols].rearrange("p (h d) -> p h d", h=kv)
                    for r in range(heads // kv):
                        out = V[:, b, r::heads // kv, t + j, 0:16]
                        last = nc.vector.tensor_copy(out, made_kv)
                last.then_inc(kept, 1)


def relative_tables(m, pe_dup, MA, MB, RAu, RBu):
    nc, tag = m.nc, m.stage("tables")
    with ExitStack() as c:
        full = m.sbuf(tag + "_pe", [P, S], F32, c)
        hi = m.sbuf(tag + "_hi", [P, S], F32R, c)
        loaded, step = m.sem(tag + "_loaded"), m.sem(tag + "_step")
        block = c.enter_context(nc.Block())

        @block.sync
        def _(sp):
            sp.dma_start(full[:], pe_dup).then_inc(loaded, 16)

        @block.vector
        def _(dve):
            dve.wait_ge(loaded, 16)
            nc.vector.tensor_copy(hi[:], full[:]).then_inc(step, 1)
            dve.wait_ge(step, 1)
            nc.vector.tensor_copy(MB[0:64, :], hi[0:64, :].bitcast(F32)).then_inc(step, 1)
            nc.vector.tensor_scalar(full[:], full[:], m.split[:, 4:5], None, ALU.mult).then_inc(step, 1)
            dve.wait_ge(step, 3)
            nc.vector.scalar_tensor_tensor(MA[:], hi[:].bitcast(F32), m.split[:, 5:6], full[:], ALU.mult,
                                           ALU.add).then_inc(step, 1)
            nc.vector.memset(RAu[:, S:S + 2].bitcast(F32), 0.0)
            nc.vector.memset(RBu[:, S:S + 2].bitcast(F32), 0.0)


def relative_operands(XT, Vall, w_rows, w_pos, MA, MB, RAl, RBl, RAu, RBu, turn, masks, ctx_out):
    def prepare(m, tag, c, normed):
        nc = m.nc
        wr = m.sbuf(tag + "_wr", [66, 256], F32, c)
        wp = m.sbuf(tag + "_wp", [16, 66 + 256], F32, c)
        comb = m.sbuf(tag + "_comb", [66, 256], F32, c)
        products = [m.sbuf(f"{tag}_products{k}", [P, 4 * BANK], F32, c) for k in range(2)]
        hi_part = [m.sbuf(f"{tag}_hi{k}", [P, 2 * BANK], F32R, c) for k in range(2)]
        x_part = [m.sbuf(f"{tag}_x{k}", [P, 2 * BANK], F32, c) for k in range(2)]
        weights_in, comb_ready, comb_done = (m.sem(tag + x) for x in ("_weights_in", "_comb_ready", "_comb_done"))
        made, halved, multiplied, content, turned_q = (
            m.sem(tag + x) for x in ("_made", "_halved", "_multiplied", "_content", "_turned_q"))
        NC = S // BANK
        ops = Operands()
        low = slice(64, P)

        def load_weights(sp, it):
            sp.dma_start(wr[:], w_rows[bass.ds(it, 1)].rearrange("a k m -> (a k) m")).then_inc(weights_in, 16)
            sp.dma_start(wp[:], w_pos[bass.ds(it, 1)].rearrange("a k m -> (a k) m")).then_inc(weights_in, 16)

        def pe_prepare(pe, it, b):
            pe.wait_ge(weights_in, 32 * (it + 1))
            nc.tensor.matmul(m.bank(7)[0:66, 0:256], wp[:, 0:66], wp[:, 66:322], start=True,
                             stop=True).then_inc(comb_ready, 1)
            pe.wait_ge(comb_done, it + 1)
            for k in range(NC):
                if k >= 2:
                    pe.wait_ge(multiplied, (it * NC + k - 1) * 4)
                    pe.wait_ge(halved, (it * NC + k - 1) * 4)
                for n, lhsT in enumerate((comb[:, 0:128], comb[:, 128:256], wr[:, 0:128], wr[:, 128:256])):
                    last = nc.tensor.matmul(m.bank((k % 2) * 4 + n), lhsT, XT[0:66, bass.ds(b * S + k * BANK, BANK)],
                                            start=True, stop=True)
                last.then_inc(made, 1)
            pe.wait_ge(content, (it + 1) * NC * 3)
            pe.wait_ge(turned_q, (it + 1) * NC * 6)

        def act_prepare(act, it):
            act.wait_ge(comb_ready, it + 1)
            nc.scalar.activation(comb[:], m.bank(7)[0:66, 0:256], ACT.Copy, scale=1 / 8).then_inc(comb_done, 1)
            for k in range(NC):
                act.wait_ge(made, it * NC + k + 1)
                if k >= 2:
                    act.wait_ge(content, (it * NC + k - 1) * 3)
                bank = m.psum[low, ((k % 2) * 4 + 2) * BANK:((k % 2) * 4 + 4) * BANK]
                for n in range(2):
                    part = slice(n * BANK, (n + 1) * BANK)
                    nc.scalar.activation(hi_part[k % 2][low, part], bank[:, part], ACT.Copy,
                                         scale=1 / 8 if n == 0 else 1.0).then_inc(halved, 1)
                    nc.scalar.activation(x_part[k % 2][low, part], bank[:, part], ACT.Copy,
                                         scale=m.split[low, 2 * n:2 * n + 1]).then_inc(halved, 1)

        def dve_prepare(dve, it):
            for k in range(NC):
                cols = slice(k * BANK, (k + 1) * BANK)
                dve.wait_ge(made, it * NC + k + 1)
                if k >= 2:
                    dve.wait_ge(turned_q, (it * NC + k - 1) * 6)
                for n in range(4):
                    nc.vector.tensor_tensor(products[k % 2][:, n * BANK:(n + 1) * BANK],
                                            m.bank((k % 2) * 4 + n % 2), turn[:, n * S + k * BANK:n * S + (k + 1) * BANK],
                                            ALU.mult).then_inc(multiplied, 1)
                dve.wait_ge(halved, (it * NC + k + 1) * 4)
                for out, n in ((RBl[low, cols], 0), (RBu[low, k * BANK + 1:(k + 1) * BANK + 1], 0), (MB[low, cols], 1)):
                    part = slice(n * BANK, (n + 1) * BANK)
                    nc.vector.scalar_tensor_tensor(out, hi_part[k % 2][low, part].bitcast(F32),
                                                   m.split[low, 2 * n + 1:2 * n + 2], x_part[k % 2][low, part],
                                                   ALU.mult, ALU.add).then_inc(content, 1)

        def pool_prepare(pool, it):
            for k in range(NC):
                cols = slice(k * BANK, (k + 1) * BANK)
                base = (it * NC + k) * 6
                pool.wait_ge(multiplied, (it * NC + k + 1) * 4)
                sums = [products[k % 2][:, n * 2 * BANK:(n * 2 + 1) * BANK] for n in range(2)]
                for n in range(2):
                    nc.gpsimd.tensor_tensor(sums[n], sums[n], products[k % 2][:, (n * 2 + 1) * BANK:(n * 2 + 2) * BANK],
                                            ALU.add).then_inc(turned_q, 1)
                pool.wait_ge(turned_q, base + 2)
                for n, RA in enumerate((RAl, RAu)):
                    nc.gpsimd.tensor_tensor(RA[:, cols], sums[n], m.split[:, 7:8].broadcast_to([P, BANK]), ALU.mult).then_inc(turned_q, 1)
                pool.wait_ge(turned_q, base + 4)
                for n, (RA, RB) in enumerate(((RAl, RBl), (RAu, RBu))):
                    nc.gpsimd.tensor_tensor(RB[0:64, cols], sums[n][0:64, :], RA[0:64, cols].bitcast(F32),
                                            ALU.subtract).then_inc(turned_q, 1)

        def pair(out, first, second, cols):
            nc.tensor.matmul(out, first, MA[:, cols], start=True, stop=False)
            return nc.tensor.matmul(out, second, MB[:, cols], start=False, stop=True)

        def scores(i, lo, hi):
            edge = min(max((i + 1) * P, lo), hi)
            q, r = slice(i * P, (i + 1) * P), slice(i * P + 1, (i + 1) * P + 1)
            if lo < edge:
                last = pair(m.psum[:, lo:edge], RAl[:, q], RBl[:, q], slice(lo, edge))
            if edge < hi:
                last = pair(m.psum[:, edge:hi], RAu[:, r], RBu[:, r], slice(edge, hi))
            return last

        def corner(i):
            return P if i == TPB - 1 else P + 2

        def diagonal(i, bank):
            q, r = slice(i * P, (i + 1) * P), slice(i * P + 1, (i + 1) * P + 1)
            pair(bank[:, 0:P], RAu[:, r], RBu[:, r], q)
            cols = slice(i * P, i * P + corner(i))
            return nc.tensor.matmul(bank[:, P:P + corner(i)], RBl[low, q], MB[low, cols], start=True, stop=True)

        def fixes(i, bank):
            n = corner(i)
            return ((i * P, (i + 1) * P, masks[:, 0:P], bank[:, 0:P]),
                    (i * P, i * P + n, masks[:, P:P + n], bank[:, P:P + n]))

        ops.weights_used, ops.uses = made, NC
        ops.load_weights, ops.pe_prepare, ops.act_prepare = load_weights, pe_prepare, act_prepare
        ops.dve_prepare, ops.pool_prepare = dve_prepare, pool_prepare
        ops.scores, ops.diagonal, ops.fixes = scores, diagonal, fixes
        ops.values_of = lambda it: Vall[:, bass.ds(it * (TPB * 32), TPB * 32)]
        ops.context = lambda b, h, j: ctx_out[:, bass.ds(b * (TPB * D) + h * 16 + j * D, 16)]
        return ops
    return prepare


def relative_constants():
    freq = np.exp(np.arange(0, D, 2, dtype=np.float32) * np.float32(-np.log(10000.0) / D)).astype(np.float64)
    t = np.arange(S, dtype=np.float64)
    angle = np.repeat(freq, 2)[:, None]
    even = (np.arange(D) % 2 == 0)[:, None]
    table = np.where(even, np.sin(angle * t), np.cos(angle * t))
    turns = []
    for a in (S - 1 - t, -(t + 1)):
        turns += [np.cos(angle * a), np.where(even, -np.sin(angle * a), np.sin(angle * a))]
    twice = lambda x: np.concatenate([x, x], 0).astype(np.float32)
    i, j = np.arange(P)[:, None], np.arange(P + 2)[None, :]
    masks = np.concatenate([j[:, :P] > i + 1, j == i + 1], 1).astype(np.int32)
    return twice(table), np.concatenate([twice(x) for x in turns], 1), masks


def swap_pairs(w):
    return w.reshape(*w.shape[:-1], -1, 2)[..., ::-1].reshape(w.shape)


def relative_weights(Wq, bq, Wk, bk, Wpos, u, v):
    rows, pos = [], []
    for h in range(4):
        s = slice(16 * h, 16 * h + 16)
        zero16 = np.zeros((66, 64), np.float32)
        q = np.concatenate([Wq[:, s], bq[None, s], u[h][None]], 0)
        k = np.concatenate([Wk[:, s], bk[None, s], np.zeros((1, 16), np.float32)], 0)
        rows.append(np.concatenate([zero16, q, q, q, q, zero16, k, k, k, k], 1))
        qv = np.concatenate([Wq[:, s], bq[None, s], v[h][None]], 0).T
        p = Wpos[:, s].T
        sw = swap_pairs(p)
        pos.append(np.concatenate([qv, p, p, sw, sw], 1))
    return np.stack(rows * B), np.stack(pos * B)


def causal_operands(XT, Vall, weights, rope, ctx_out):
    def prepare(m, tag, c, normed):
        nc = m.nc
        w = m.sbuf(tag + "_wqk", [D + 2, 4 * D], F32, c)
        products = [m.sbuf(f"{tag}_products{k}", [D, 4 * BANK], F32, c) for k in range(2)]
        hi_part = [m.sbuf(f"{tag}_hi{k}", [D, 2 * BANK], F32R, c) for k in range(2)]
        x_part = [m.sbuf(f"{tag}_x{k}", [D, 2 * BANK], F32, c) for k in range(2)]
        QS, KS = (m.sbuf(tag + n, [D, S], F32R, c) for n in ("_QS", "_KS"))
        weights_in, made, halved, multiplied, content, summed = (
            m.sem(tag + x) for x in ("_weights_in", "_made", "_halved", "_multiplied", "_content", "_summed"))
        NC = S // BANK
        ops = Operands()

        def load_weights(sp, it):
            sp.dma_start(w[:], weights[bass.ds(it, 1)].rearrange("a k m -> (a k) m")).then_inc(weights_in, 16)

        def pe_prepare(pe, it, b):
            pe.wait_ge(weights_in, 16 * (it + 1))
            for k in range(NC):
                if k >= 2:
                    pe.wait_ge(multiplied, (it * NC + k - 1) * 4)
                for n in range(4):
                    last = nc.tensor.matmul(m.bank((k % 2) * 4 + n)[0:D, :], w[:, n * D:(n + 1) * D],
                                            XT[:, bass.ds(b * S + k * BANK, BANK)], start=True, stop=True)
                last.then_inc(made, 1)
            pe.wait_ge(content, (it + 1) * NC * 2)

        def dve_prepare(dve, it):
            for k in range(NC):
                cols = slice(k * BANK, (k + 1) * BANK)
                dve.wait_ge(made, it * NC + k + 1)
                if k >= 2:
                    dve.wait_ge(halved, (it * NC + k - 1) * 4)
                for n in range(4):
                    nc.vector.tensor_tensor(products[k % 2][:, n * BANK:(n + 1) * BANK],
                                            m.bank((k % 2) * 4 + n)[0:D, :],
                                            rope[:, (n % 2) * S + k * BANK:(n % 2) * S + (k + 1) * BANK],
                                            ALU.mult).then_inc(multiplied, 1)
                dve.wait_ge(halved, (it * NC + k + 1) * 4)
                for n, out in enumerate((QS, KS)):
                    part = slice(n * BANK, (n + 1) * BANK)
                    nc.vector.scalar_tensor_tensor(out[:, cols], hi_part[k % 2][:, part].bitcast(F32),
                                                   m.split[0:D, 2 * n + 1:2 * n + 2], x_part[k % 2][:, part],
                                                   ALU.mult, ALU.add).then_inc(content, 1)

        def pool_prepare(pool, it):
            for k in range(NC):
                pool.wait_ge(multiplied, (it * NC + k + 1) * 4)
                for n in range(2):
                    first, second = (products[k % 2][:, (2 * n + r) * BANK:(2 * n + r + 1) * BANK] for r in range(2))
                    nc.gpsimd.tensor_tensor(first, first, second, ALU.add).then_inc(summed, 1)

        def act_prepare(act, it):
            for k in range(NC):
                act.wait_ge(summed, (it * NC + k + 1) * 2)
                if k >= 2:
                    act.wait_ge(content, (it * NC + k - 1) * 2)
                for n, factor in enumerate((6, 2)):
                    part, whole = slice(n * BANK, (n + 1) * BANK), products[k % 2][:, 2 * n * BANK:(2 * n + 1) * BANK]
                    nc.scalar.activation(hi_part[k % 2][:, part], whole, ACT.Copy,
                                         scale=1 / 4 if n == 0 else 1.0).then_inc(halved, 1)
                    nc.scalar.activation(x_part[k % 2][:, part], whole, ACT.Copy,
                                         scale=m.split[0:D, factor:factor + 1]).then_inc(halved, 1)

        def scores(i, lo, hi):
            return nc.tensor.matmul(m.psum[:, lo:hi], QS[:, i * P:(i + 1) * P], KS[:, lo:hi], start=True, stop=True)

        ops.weights_used, ops.uses = made, NC
        ops.load_weights, ops.pe_prepare, ops.act_prepare = load_weights, pe_prepare, act_prepare
        ops.dve_prepare, ops.pool_prepare, ops.scores = dve_prepare, pool_prepare, scores
        ops.values_of = lambda it: Vall[:, bass.ds(it * (TPB * 32), TPB * 32)]
        ops.context = lambda b, h, j: ctx_out[:, bass.ds(b * (TPB * D) + h * 16 + j * D, 16)]
        return ops
    return prepare


def wide_values(m, XT, weight, values_dram):
    nc, tag = m.nc, m.stage("values")
    cols, PER = 8 * D, 4
    groups = NT // PER
    with ExitStack() as c:
        w = m.sbuf(tag + "_w", [D, cols], F32, c)
        staged = [m.sbuf(f"{tag}_staged{k}", [P, PER * cols], F32, c) for k in range(2)]
        loaded, made, kept_v, kept_s = (m.sem(tag + x) for x in ("_loaded", "_made", "_kept_v", "_kept_s"))
        stored = [m.sem(f"{tag}_stored{k}") for k in range(2)]
        block = c.enter_context(nc.Block())

        def copied_to(g, j):
            return staged[g % 2][:].rearrange("p (h t d) -> p h t d", h=8, t=PER)[:, :, j, :]

        @block.sync
        def _(sp):
            sp.dma_start(w[:], weight).then_inc(loaded, 16)
            for g in range(groups):
                sp.wait_ge(kept_v, 2 * (g + 1))
                sp.wait_ge(kept_s, 2 * (g + 1))
                b, t = g * PER // TPB, g * PER % TPB
                sp.dma_start(values_dram[b * 8:(b + 1) * 8, :, t * D:(t + PER) * D].rearrange("h p n -> p h n"),
                             staged[g % 2][:].rearrange("p (h n) -> p h n", h=8)).then_inc(stored[g % 2], 16)
            for k in range(2):
                sp.wait_ge(stored[k], 16 * (groups // 2))

        @block.tensor
        def _(pe):
            pe.wait_ge(loaded, 16)
            for t in range(NT):
                if t >= 4:
                    pe.wait_ge(kept_s if t % 2 else kept_v, (t - 4) // 2 + 1)
                nc.tensor.matmul(m.bank(t % 4), XT[0:D, t * P:(t + 1) * P], w[:], start=True, stop=True).then_inc(made, 1)

        @block.vector
        def _(dve):
            for t in range(0, NT, 2):
                dve.wait_ge(made, t + 1)
                g, j = t // PER, t % PER
                if g >= 2 and j == 0:
                    dve.wait_ge(stored[g % 2], 16 * (g // 2))
                nc.vector.tensor_copy(copied_to(g, j), m.bank(t % 4).rearrange("p (h d) -> p h d", h=8)).then_inc(kept_v, 1)

        @block.scalar
        def _(act):
            for t in range(1, NT, 2):
                act.wait_ge(made, t + 1)
                g, j = t // PER, t % PER
                if g >= 2 and j == 1:
                    act.wait_ge(stored[g % 2], 16 * (g // 2))
                nc.scalar.activation(copied_to(g, j), m.bank(t % 4).rearrange("p (h d) -> p h d", h=8),
                                     ACT.Copy).then_inc(kept_s, 1)


def wide_operands(XT, values_dram, weights, ctx_out):
    def prepare(m, tag, c, normed):
        nc = m.nc
        w = m.sbuf(tag + "_wqk", [D, 4 * D], F32, c)
        hi_part = [m.sbuf(f"{tag}_hi{k}", [P, BANK], F32R, c) for k in range(2)]
        x_part = [m.sbuf(f"{tag}_x{k}", [P, 2 * BANK], F32, c) for k in range(2)]
        QH, QL, KS = (m.sbuf(tag + n, [P, S], F32R, c) for n in ("_QH", "_QL", "_KS"))
        weights_in, made, halved, content, queries = (
            m.sem(tag + x) for x in ("_weights_in", "_made", "_halved", "_content", "_queries"))
        NC = S // BANK
        scale = float(np.float32(1) / np.float32(np.sqrt(8)))
        ops = Operands()

        def load_weights(sp, it):
            sp.dma_start(w[:], weights[bass.ds(it, 1)].rearrange("a k m -> (a k) m")).then_inc(weights_in, 16)

        def pe_prepare(pe, it, b):
            pe.wait_ge(weights_in, 16 * (it + 1))
            for k in range(NC):
                for n in range(2):
                    last = nc.tensor.matmul(m.bank(2 * k + n), w[:, n * P:(n + 1) * P],
                                            XT[0:D, bass.ds(b * S + k * BANK, BANK)], start=True, stop=True)
                last.then_inc(made, 1)
            pe.wait_ge(content, (it + 1) * NC)
            pe.wait_ge(queries, (it + 1) * NC * 2)

        def act_prepare(act, it):
            for k in range(NC):
                act.wait_ge(made, it * NC + k + 1)
                if k >= 2:
                    act.wait_ge(content, it * NC + k - 1)
                    act.wait_ge(queries, (it * NC + k - 1) * 2)
                nc.scalar.activation(x_part[k % 2][:, 0:BANK], m.bank(2 * k), ACT.Copy, scale=scale).then_inc(halved, 1)
                nc.scalar.activation(hi_part[k % 2][:], m.bank(2 * k + 1), ACT.Copy).then_inc(halved, 1)
                nc.scalar.activation(x_part[k % 2][:, BANK:], m.bank(2 * k + 1), ACT.Copy,
                                     scale=m.split[:, 4:5]).then_inc(halved, 1)

        def dve_prepare(dve, it):
            for k in range(NC):
                dve.wait_ge(halved, (it * NC + k + 1) * 3)
                nc.vector.scalar_tensor_tensor(KS[:, k * BANK:(k + 1) * BANK], hi_part[k % 2][:].bitcast(F32),
                                               m.split[:, 5:6], x_part[k % 2][:, BANK:], ALU.mult,
                                               ALU.add).then_inc(content, 1)

        def pool_prepare(pool, it):
            for k in range(NC):
                cols = slice(k * BANK, (k + 1) * BANK)
                pool.wait_ge(halved, (it * NC + k) * 3 + 1)
                nc.gpsimd.tensor_tensor(QH[:, cols], x_part[k % 2][:, 0:BANK],
                                        m.split[:, 7:8].broadcast_to([P, BANK]), ALU.mult).then_inc(queries, 1)
                pool.wait_ge(queries, (it * NC + k) * 2 + 1)
                nc.gpsimd.tensor_tensor(QL[:, cols], x_part[k % 2][:, 0:BANK], QH[:, cols].bitcast(F32),
                                        ALU.subtract).then_inc(queries, 1)

        def scores(i, lo, hi):
            q = slice(i * P, (i + 1) * P)
            nc.tensor.matmul(m.psum[:, lo:hi], QH[:, q], KS[:, lo:hi], start=True, stop=False)
            return nc.tensor.matmul(m.psum[:, lo:hi], QL[:, q], KS[:, lo:hi], start=False, stop=True)

        ops.weights_used, ops.uses = made, NC
        ops.load_weights, ops.pe_prepare, ops.act_prepare = load_weights, pe_prepare, act_prepare
        ops.dve_prepare, ops.pool_prepare, ops.scores = dve_prepare, pool_prepare, scores
        ops.values_of = lambda it: values_dram[bass.ds(it, 1)].rearrange("a p n -> (a p) n")
        ops.context = lambda b, h, j: ctx_out[:, bass.ds((b * TPB + j) * (8 * D) + h * D, D)]
        return ops
    return prepare


def project_wide(m, ctx, weight, bias, dst):
    nc, tag = m.nc, m.stage("outw")
    PIECES = 8 * D // P
    with ExitStack() as c:
        w = m.sbuf(tag + "_w", [P, PIECES * D], F32, c)
        b_all = m.sbuf(tag + "_bias", [P, D], F32, c)
        turnedT = [m.sbuf(f"{tag}_ctxT{k}", [P, PIECES * P], F32, c) for k in range(2)]
        loaded, turned, copied, made, added, biased = (
            m.sem(tag + x) for x in ("_loaded", "_turned", "_copied", "_made", "_added", "_biased"))
        block = c.enter_context(nc.Block())

        @block.sync
        def _(sp):
            sp.dma_start(w[:].rearrange("p (q d) -> p q d", q=PIECES),
                         weight.rearrange("(q p) d -> p q d", p=P)).then_inc(loaded, 16)
            sp.dma_start(b_all[:], bias.partition_broadcast(P)).then_inc(loaded, 16)

        @block.tensor
        def _(pe):
            pe.wait_ge(loaded, 32)
            for step in range(NT + 1):
                if step < NT:
                    if step >= 2:
                        pe.wait_ge(copied, step - 1)
                    for q in range(PIECES):
                        last = nc.tensor.transpose(m.bank(step % 2)[:, q * P:(q + 1) * P],
                                                   ctx[:, (step * PIECES + q) * P:(step * PIECES + q + 1) * P],
                                                   m.ident[:])
                    last.then_inc(turned, 1)
                t = step - 1
                if t >= 0:
                    pe.wait_ge(copied, t + 1)
                    if t >= 2:
                        pe.wait_ge(added, t - 1)
                    for q in range(PIECES):
                        last = nc.tensor.matmul(m.bank(2 + t % 2)[:, 0:D], turnedT[t % 2][:, q * P:(q + 1) * P],
                                                w[:, q * D:(q + 1) * D], start=q == 0, stop=q == PIECES - 1)
                    last.then_inc(made, 1)

        @block.scalar
        def _(act):
            for t in range(NT):
                act.wait_ge(turned, t + 1)
                if t >= 2:
                    act.wait_ge(made, t - 1)
                nc.scalar.activation(turnedT[t % 2][:], m.bank(t % 2), ACT.Copy).then_inc(copied, 1)

        @block.vector
        def _(dve):
            dve.wait_ge(loaded, 32)
            nc.vector.tensor_tensor(tiles(dst), tiles(dst), bcast(b_all[:], [P, NT, D], 1), ALU.add).then_inc(biased, 1)
            dve.wait_ge(biased, 1)
            for t in range(NT):
                dve.wait_ge(made, t + 1)
                nc.vector.tensor_tensor(dst[:, t * D:(t + 1) * D], m.bank(2 + t % 2)[:, 0:D],
                                        dst[:, t * D:(t + 1) * D], ALU.add).then_inc(added, 1)


def split_channels(m, src, FS):
    nc, tag = m.nc, m.stage("split")
    PER = BANK // P
    groups = NT // PER
    with ExitStack() as c:
        hi = [m.sbuf(f"{tag}_hi{k}", [P, BANK], F32R, c) for k in range(2)]
        x = [m.sbuf(f"{tag}_x{k}", [P, BANK], F32, c) for k in range(2)]
        twice = m.sbuf(tag + "_twice", [P, 2 * NT * D], F32, c)
        doubled, turned, halved, scaled, joined = (
            m.sem(tag + n) for n in ("_doubled", "_turned", "_halved", "_scaled", "_joined"))
        block = c.enter_context(nc.Block())

        @block.gpsimd
        def _(pool):
            for g in range(groups):
                out = twice[:, g * 2 * PER * D:(g + 1) * 2 * PER * D].rearrange("p (t r d) -> p t r d", t=PER, r=2)
                one = src[:, g * PER * D:(g + 1) * PER * D].rearrange("p (t d) -> p t d", t=PER)
                nc.gpsimd.tensor_copy(out, bcast(one, [P, PER, 2, D], 2)).then_inc(doubled, 1)

        @block.tensor
        def _(pe):
            for g in range(groups):
                pe.wait_ge(doubled, g + 1)
                if g >= 2:
                    pe.wait_ge(halved, g - 1)
                    pe.wait_ge(scaled, g - 1)
                for j in range(PER):
                    t = g * PER + j
                    last = nc.tensor.transpose(m.bank(g % 2)[:, j * P:(j + 1) * P],
                                               twice[:, t * 2 * D:(t + 1) * 2 * D], m.ident[:])
                last.then_inc(turned, 1)

        @block.scalar
        def _(act):
            for g in range(groups):
                act.wait_ge(turned, g + 1)
                if g >= 2:
                    act.wait_ge(joined, g - 1)
                nc.scalar.activation(hi[g % 2][:], m.bank(g % 2), ACT.Copy).then_inc(halved, 1)

        @block.vector
        def _(dve):
            for g in range(groups):
                dve.wait_ge(halved, g + 1)
                if g >= 2:
                    dve.wait_ge(joined, g - 1)
                nc.vector.tensor_scalar(x[g % 2][:], m.bank(g % 2), m.split[:, 4:5], None, ALU.mult).then_inc(scaled, 1)
                dve.wait_ge(scaled, g + 1)
                nc.vector.scalar_tensor_tensor(FS[:, g * BANK:(g + 1) * BANK], hi[g % 2][:].bitcast(F32),
                                               m.split[:, 5:6], x[g % 2][:], ALU.mult, ALU.add).then_inc(joined, 1)


def split_weights(m, source, hi, lo):
    nc, tag = m.nc, m.stage("wsplit")
    with ExitStack() as c:
        full = m.sbuf(tag + "_full", [P, hi.shape[1]], F32, c)
        loaded, step = m.sem(tag + "_loaded"), m.sem(tag + "_step")
        block = c.enter_context(nc.Block())

        @block.sync
        def _(sp):
            sp.dma_start(full[0:D, :], source).then_inc(loaded, 16)
            sp.dma_start(full[D:P, :], source).then_inc(loaded, 16)

        @block.vector
        def _(dve):
            dve.wait_ge(loaded, 32)
            nc.vector.tensor_copy(hi[:], full[:]).then_inc(step, 1)
            dve.wait_ge(step, 1)
            nc.vector.tensor_tensor(lo[:], full[:], hi[:].bitcast(F32), ALU.subtract).then_inc(step, 1)


def route(m, FS, r_hi, r_lo, bias, before, gates):
    nc, tag = m.nc, m.stage("route")
    probs_first = bias is None
    with ExitStack() as c:
        logits, expo = (m.sbuf(tag + n, [P, NT * E], F32, c) for n in ("_logits", "_expo"))
        more, same = (m.sbuf(tag + n, [P, NT * E * E], F32, c) for n in ("_more", "_same"))
        rank = m.sbuf(tag + "_rank", [P, NT * E], F32, c)
        stat = m.sbuf(tag + "_stat", [P, 2 * NT], F32, c)
        order = m.sbuf(tag + "_order", [P, E * E + E], F32, c)
        loaded, made, step, raised = (m.sem(tag + n) for n in ("_loaded", "_made", "_step", "_raised"))
        block = c.enter_context(nc.Block())
        top, total = stat[:, 0:NT], stat[:, NT:2 * NT]
        by_e = lambda t: t[:].rearrange("p (t e) -> p t e", e=E)
        pairs = lambda t: t[:].rearrange("p (t e f) -> p t e f", e=E, f=E)
        shape, shape4 = [P, NT, E], [P, NT, E, E]

        @block.sync
        def _(sp):
            sp.dma_start(order[:, 0:E * E], before.partition_broadcast(P)).then_inc(loaded, 16)
            if bias is not None:
                sp.dma_start(order[:, E * E:], bias.partition_broadcast(P)).then_inc(loaded, 16)

        @block.tensor
        def _(pe):
            for t in range(NT):
                out = m.bank(0)[:, t * E:(t + 1) * E]
                nc.tensor.matmul(out, FS[:, t * P:(t + 1) * P], r_hi, start=True, stop=False)
                last = nc.tensor.matmul(out, FS[:, t * P:(t + 1) * P], r_lo, start=False, stop=True)
            last.then_inc(made, 1)

        @block.scalar
        def _(act):
            act.wait_ge(step, 3)
            nc.scalar.activation(expo[:], expo[:], ACT.Exp).then_inc(raised, 1)

        @block.vector
        def _(dve):
            n = 0

            def done(instruction):
                nonlocal n
                n += 1
                instruction.then_inc(step, 1)
                dve.wait_ge(step, n)

            dve.wait_ge(made, 1)
            dve.wait_ge(loaded, 16 if probs_first else 32)
            if probs_first:
                done(nc.vector.tensor_copy(logits[:], m.bank(0)[:, 0:NT * E]))
            else:
                done(nc.vector.tensor_tensor(by_e(logits), m.bank(0)[:, 0:NT * E].rearrange("p (t e) -> p t e", e=E),
                                             bcast(order[:, E * E:], shape, 1), ALU.add))
            done(nc.vector.tensor_reduce(top, by_e(logits), axis=AX.X, op=ALU.max))
            done(nc.vector.tensor_tensor(by_e(expo), by_e(logits), bcast(top, shape, 2), ALU.subtract))
            dve.wait_ge(raised, 1)
            ranked = logits
            if probs_first:
                done(nc.vector.tensor_reduce(total, by_e(expo), axis=AX.X, op=ALU.add))
                done(nc.vector.reciprocal(total, total))
                done(nc.vector.tensor_tensor(by_e(expo), by_e(expo), bcast(total, shape, 2), ALU.mult))
                ranked = expo
            others, own = bcast(by_e(ranked), shape4, 2), bcast(by_e(ranked), shape4, 3)
            done(nc.vector.tensor_tensor(pairs(more), others, own, ALU.is_gt))
            done(nc.vector.tensor_tensor(pairs(same), others, own, ALU.is_equal))
            flat = lambda t: t[:].rearrange("p (t n) -> p t n", t=NT)
            done(nc.vector.tensor_tensor(flat(same), flat(same), bcast(order[:, 0:E * E], [P, NT, E * E], 1), ALU.mult))
            done(nc.vector.tensor_tensor(more[:], more[:], same[:], ALU.add))
            done(nc.vector.tensor_reduce(by_e(rank), pairs(more), axis=AX.X, op=ALU.add))
            done(nc.vector.tensor_scalar(rank[:], rank[:], 1.5, None, ALU.is_lt))
            done(nc.vector.tensor_tensor(expo[:], expo[:], rank[:], ALU.mult))
            done(nc.vector.tensor_reduce(total, by_e(expo), axis=AX.X, op=ALU.add))
            if probs_first:
                done(nc.vector.tensor_scalar(total, total, 1e-9, None, ALU.add))
            done(nc.vector.reciprocal(total, total))
            done(nc.vector.tensor_tensor(by_e(gates), by_e(expo), bcast(total, shape, 2), ALU.mult))


HID = int(8 / 3 * D)
REST = HID - P
GATED_COLS = 2 * P + D + REST


def mix_gated(m, FS, w_hi, w_lo, down, gates, dst):
    nc, tag = m.nc, m.stage("gated")
    CH = 2 * P
    with ExitStack() as c:
        hidden = [m.sbuf(f"{tag}_hidden{k}", [P, 2 * CH], F32, c) for k in range(2)]
        act_part = [m.sbuf(f"{tag}_act{k}", [P, 2 * CH], F32, c) for k in range(2)]
        w_down = m.sbuf(tag + "_down", [P, 2 * E * D], F32, c)
        weighted = m.sbuf(tag + "_weighted", [P, E * D], F32, c)
        summed = m.sbuf(tag + "_summed", [P, D], F32, c)
        loaded, made, silu, ready, used, out_read, mix_step = (
            m.sem(tag + n) for n in "_loaded _made _silu _ready _used _out_read _mix_step".split())
        block = c.enter_context(nc.Block())
        NCH = N // CH
        view = lambda t: t[:].rearrange("p (e d) -> p e d", e=E)

        @block.sync
        def _(sp):
            sp.dma_start(w_down[:, 0:E * D], down[0:P, :]).then_inc(loaded, 16)
            sp.dma_start(w_down[0:REST, E * D:], down[P:HID, :]).then_inc(loaded, 16)

        @block.tensor
        def _(pe):
            pe.wait_ge(loaded, 32)
            with pe.Fori(0, NCH) as n:
                tokens = bass.ds(n * CH, CH)
                for step in range(E + 1):
                    e = step
                    if e < E:
                        k = e % 2
                        if e >= 2:
                            pe.wait_ge(ready, (n * E + e - 1) * 2)
                        base = e * GATED_COLS
                        for out, lo, wid in ((m.bank(2 * k)[:, 0:CH], 0, P), (m.bank(2 * k)[:, CH:], P, P),
                                             (m.bank(2 * k + 1)[0:D + REST, 0:CH], 2 * P, D + REST)):
                            nc.tensor.matmul(out, w_hi[:, base + lo:base + lo + wid], FS[:, tokens], start=True, stop=False)
                            last = nc.tensor.matmul(out, w_lo[:, base + lo:base + lo + wid], FS[:, tokens],
                                                    start=False, stop=True)
                        last.then_inc(made, 1)
                    e = step - 1
                    if e >= 0:
                        k = e % 2
                        pe.wait_ge(ready, (n * E + e + 1) * 2)
                        for t in range(2):
                            out = m.bank(4 + t)[:, e * D:(e + 1) * D]
                            nc.tensor.matmul(out, hidden[k][:, t * P:(t + 1) * P], w_down[:, e * D:(e + 1) * D],
                                             start=True, stop=False)
                            last = nc.tensor.matmul(out, hidden[k][0:REST, CH + t * P:CH + (t + 1) * P],
                                                    w_down[0:REST, (E + e) * D:(E + e + 1) * D], start=False, stop=True)
                        last.then_inc(used, 1)
                pe.wait_ge(out_read, (n + 1) * 2)

        @block.scalar
        def _(act):
            with act.Fori(0, NCH) as n:
                for e in range(E):
                    k = e % 2
                    act.wait_ge(made, n * E + e + 1)
                    if e >= 2:
                        act.wait_ge(ready, (n * E + e - 1) * 2)
                    nc.scalar.activation(act_part[k][:, 0:CH], m.bank(2 * k)[:, 0:CH], ACT.Silu).then_inc(silu, 1)
                    nc.scalar.activation(act_part[k][0:REST, CH:], m.bank(2 * k + 1)[0:REST, 0:CH],
                                         ACT.Silu).then_inc(silu, 1)

        @block.vector
        def _(dve):
            with dve.Fori(0, NCH) as n:
                for e in range(E):
                    k = e % 2
                    if e >= 2:
                        dve.wait_ge(used, n * E + e - 1)
                    dve.wait_ge(silu, (n * E + e) * 2 + 1)
                    nc.vector.tensor_tensor(hidden[k][:, 0:CH], act_part[k][:, 0:CH], m.bank(2 * k)[:, CH:],
                                            ALU.mult).then_inc(ready, 1)
                    dve.wait_ge(silu, (n * E + e) * 2 + 2)
                    nc.vector.tensor_tensor(hidden[k][0:REST, CH:], act_part[k][0:REST, CH:],
                                            m.bank(2 * k + 1)[D:D + REST, 0:CH], ALU.mult).then_inc(ready, 1)
                dve.wait_ge(used, (n + 1) * E)
                mix_outputs(m, dve, n, 4, gates, weighted, summed, dst, out_read, mix_step)


def mix_outputs(m, dve, n, bank0, gates, weighted, summed, dst, out_read, mix_step):
    nc = m.nc
    view = lambda t: t.rearrange("p (e d) -> p e d", e=E)
    for t in range(2):
        base = (n * 2 + t) * 3
        gate = gates[:, bass.ds((n * 2 + t) * E, E)]
        nc.vector.tensor_tensor(view(weighted[:]), view(m.bank(bank0 + t)), bcast(gate, [P, E, D], 2),
                                ALU.mult).then_inc(out_read, 1)
        dve.wait_ge(out_read, n * 2 + t + 1)
        nc.vector.tensor_reduce(summed[:], weighted[:].rearrange("p (e d) -> p d e", e=E), axis=AX.X,
                                op=ALU.add).then_inc(mix_step, 1)
        dve.wait_ge(mix_step, (n * 2 + t) * 2 + 1)
        own = dst[:, bass.ds((n * 2 + t) * D, D)]
        nc.vector.tensor_tensor(own, own, summed[:], ALU.add).then_inc(mix_step, 1)
        dve.wait_ge(mix_step, (n * 2 + t) * 2 + 2)


def mix_gelu(m, FS, w_hi, w_lo, b1, down, b2, gates, dst):
    nc, tag = m.nc, m.stage("gelu")
    CH = 2 * P
    with ExitStack() as c:
        hidden = [m.sbuf(f"{tag}_hidden{k}", [P, CH], F32, c) for k in range(2)]
        w_down = m.sbuf(tag + "_down", [P, E * D], F32, c)
        b1_col = m.sbuf(tag + "_b1", [P, E], F32, c)
        b2_row = m.sbuf(tag + "_b2", [1, E * D], F32, c)
        ones = m.sbuf(tag + "_ones", [1, P], F32, c)
        weighted = m.sbuf(tag + "_weighted", [P, E * D], F32, c)
        summed = m.sbuf(tag + "_summed", [P, D], F32, c)
        loaded, made, raised, used, out_read, mix_step, one_in = (
            m.sem(tag + n) for n in "_loaded _made _raised _used _out_read _mix_step _one".split())
        block = c.enter_context(nc.Block())
        NCH = N // CH

        @block.sync
        def _(sp):
            sp.dma_start(w_down[:].rearrange("p (e d) -> p e d", e=E), down.rearrange("e h d -> h e d")).then_inc(loaded, 16)
            sp.dma_start(b1_col[:], b1).then_inc(loaded, 16)
            sp.dma_start(b2_row[:], b2).then_inc(loaded, 16)

        @block.gpsimd
        def _(pool):
            nc.gpsimd.memset(ones[:], 1.0).then_inc(one_in, 1)

        @block.tensor
        def _(pe):
            pe.wait_ge(loaded, 48)
            pe.wait_ge(one_in, 1)
            with pe.Fori(0, NCH) as n:
                tokens = bass.ds(n * CH, CH)
                for step in range(E + 1):
                    e = step
                    if e < E:
                        if e >= 2:
                            pe.wait_ge(raised, n * E + e - 1)
                        out = m.bank(e % 2)[:, 0:CH]
                        nc.tensor.matmul(out, w_hi[:, e * P:(e + 1) * P], FS[:, tokens], start=True, stop=False)
                        nc.tensor.matmul(out, w_lo[:, e * P:(e + 1) * P], FS[:, tokens], start=False,
                                         stop=True).then_inc(made, 1)
                    e = step - 1
                    if e >= 0:
                        pe.wait_ge(raised, n * E + e + 1)
                        for t in range(2):
                            out = m.bank(4 + t)[:, e * D:(e + 1) * D]
                            nc.tensor.matmul(out, hidden[e % 2][:, t * P:(t + 1) * P], w_down[:, e * D:(e + 1) * D],
                                             start=True, stop=False)
                            last = nc.tensor.matmul(out, ones[:], b2_row[0:1, e * D:(e + 1) * D], start=False, stop=True)
                        last.then_inc(used, 1)
                pe.wait_ge(out_read, (n + 1) * 2)

        @block.scalar
        def _(act):
            act.wait_ge(loaded, 48)
            with act.Fori(0, NCH) as n:
                for e in range(E):
                    act.wait_ge(made, n * E + e + 1)
                    if e >= 2:
                        act.wait_ge(used, n * E + e - 1)
                    nc.scalar.activation(hidden[e % 2][:], m.bank(e % 2)[:, 0:CH], ACT.Gelu,
                                         bias=b1_col[:, e:e + 1]).then_inc(raised, 1)

        @block.vector
        def _(dve):
            with dve.Fori(0, NCH) as n:
                dve.wait_ge(used, (n + 1) * E)
                mix_outputs(m, dve, n, 4, gates, weighted, summed, dst, out_read, mix_step)


def add(m, dst, src):
    nc, half = m.nc, NT * D // 2
    with nc.Block() as block:
        @block.vector
        def _(dve):
            nc.vector.tensor_tensor(dst[:, 0:half], dst[:, 0:half], src[:, 0:half], ALU.add)

        @block.gpsimd
        def _(pool):
            nc.gpsimd.tensor_tensor(dst[:, half:], dst[:, half:], src[:, half:], ALU.add)


def load(m, pairs):
    nc, loaded = m.nc, m.sem(m.stage("load"))
    with nc.Block() as block:
        @block.sync
        def _(sp):
            for sb, dram in pairs:
                sp.dma_start(sb, dram).then_inc(loaded, 16)
            sp.wait_ge(loaded, 16 * len(pairs))


def tower(nc, a, out):
    whole = ExitStack()
    with whole:
        m = Machine(nc, whole)
        m.psum = whole.enter_context(nc.psum_tensor("psum", [P, 8 * BANK], F32))
        m.bank = lambda k: m.psum[:, k * BANK:(k + 1) * BANK]
        m.H = m.sbuf("H", [P, NT * D])
        m.ident, m.split = m.sbuf("ident_sb", [P, P]), m.sbuf("split_sb", [P, 8])
        m.join = {w: m.sbuf(f"join{w}_sb", [P, w]) for w in (32, 64)}
        m.causal_mask = m.sbuf("causal_mask_sb", [P, P])
        X, Y = m.sbuf("X", [P, NT * D]), m.sbuf("Y", [P, NT * D])
        load(m, [(m.ident[:], a["ident"]), (m.split[:], a["split"]), (m.join[32][:], a["join32"]),
                 (m.join[64][:], a["join64"]), (m.causal_mask[:], a["causal_mask"])])
        embed(m, a["tokens"], a["token_W"], a["pe_rows"], a["iota"])

        normalize(m, m.H, X, LN_EPS)
        normalize(m, X, X, LN_EPS, gamma=a["ln_gamma"], beta=a["ln_beta"])
        with ExitStack() as c:
            XT = m.sbuf("XT0", [D + 2, N], F32, c)
            channels_first(m, X, XT, ones=2)
            Vall = m.sbuf("Vall0", [P, B * 4 * TPB * 32], F32, c)
            all_values(m, XT, D + 2, a["rel_v"], "relative", Vall)
            with ExitStack() as c2:
                MA, MB, RAl, RBl = (m.sbuf(n, [P, S], F32R, c2) for n in ("MA", "MB", "RAl", "RBl"))
                RAu, RBu = (m.sbuf(n, [P, S + 2], F32R, c2) for n in ("RAu", "RBu"))
                turn, masks = m.sbuf("turn", [P, 4 * S], F32, c2), m.sbuf("masks", [P, 2 * P + 2], I32, c2)
                load(m, [(turn[:], a["turns"]), (masks[:], a["rel_masks"])])
                relative_tables(m, a["pe_table"], MA, MB, RAu, RBu)
                attention(m, "relative", 4, 16, relative_operands(XT, Vall, a["rel_rows"], a["rel_pos"], MA, MB,
                                                                  RAl, RBl, RAu, RBu, turn, masks, Y), spare=X)
            channels_first(m, Y, XT, ones=1)
            project_add(m, XT, D + 1, a["rel_out"], m.H)

        m.renew_semaphores()

        normalize(m, m.H, X, LN_EPS)
        normalize(m, X, Y, RMS_EPS, mean=False, gamma=a["ln1_w"])
        with ExitStack() as c:
            XT = m.sbuf("XT1", [D + 2, N], F32, c)
            channels_first(m, Y, XT, ones=2)
            Vall = m.sbuf("Vall1", [P, B * 4 * TPB * 32], F32, c)
            all_values(m, XT, D, a["causal_v"], "causal", Vall)
            rope = m.sbuf("rope", [D, 2 * S], F32, c)
            load(m, [(rope[:], a["rope_table"])])
            attention(m, "causal", 4, 16, causal_operands(XT, Vall, a["causal_qk"], rope, Y))
            channels_first(m, Y, XT)
            project_add(m, XT, D, a["causal_out"], X)
        normalize(m, X, Y, RMS_EPS, mean=False, gamma=a["ln2_w"])
        add(m, m.H, X)
        with ExitStack() as c:
            FS = m.sbuf("FS0", [P, N], F32R, c)
            split_channels(m, Y, FS)
            cols = E * GATED_COLS
            w_hi, w_lo = (m.sbuf(n, [P, cols], F32R, c) for n in ("gated_hi", "gated_lo"))
            r_hi, r_lo = (m.sbuf(n, [P, E], F32R, c) for n in ("router0_hi", "router0_lo"))
            split_weights(m, a["gated_up"], w_hi, w_lo)
            split_weights(m, a["router0"], r_hi, r_lo)
            gates = m.sbuf("gates0", [P, NT * E], F32, c)
            route(m, FS, r_hi[:], r_lo[:], None, a["before"], gates)
            mix_gated(m, FS, w_hi, w_lo, a["gated_down"], gates, m.H)

        m.renew_semaphores()

        normalize(m, m.H, X, LN_EPS)
        with ExitStack() as c:
            CTX = m.sbuf("CTX", [P, NT * 8 * D], F32, c)
            with ExitStack() as c2:
                XT = m.sbuf("XT2", [D, N], F32, c2)
                channels_first(m, X, XT)
                values = nc.dram_tensor("wide_values", [B * 8, P, TPB * D], F32).ap()
                wide_values(m, XT, a["wide_v"], values)
                attention(m, "wide", 8, D, wide_operands(XT, values, a["wide_qk"], CTX))
            project_wide(m, CTX, a["wide_out"], a["wide_bout"], m.H)

        normalize(m, m.H, X, LN_EPS)
        normalize(m, X, X, LN_EPS, gamma=a["gamma1"], beta=a["beta1"])
        with ExitStack() as c:
            FS = m.sbuf("FS1", [P, N], F32R, c)
            split_channels(m, X, FS)
            w_hi, w_lo = (m.sbuf(n, [P, E * P], F32R, c) for n in ("gelu_hi", "gelu_lo"))
            r_hi, r_lo = (m.sbuf(n, [P, E], F32R, c) for n in ("router1_hi", "router1_lo"))
            split_weights(m, a["gelu_up"], w_hi, w_lo)
            split_weights(m, a["router1"], r_hi, r_lo)
            gates = m.sbuf("gates1", [P, NT * E], F32, c)
            route(m, FS, r_hi[:], r_lo[:], a["router1_bias"], a["before"], gates)
            mix_gelu(m, FS, w_hi, w_lo, a["gelu_b1"], a["gelu_down"], a["gelu_b2"], gates, m.H)
        stored = m.sem("stored")
        with nc.Block() as block:
            @block.sync
            def _(sp):
                sp.dma_start(out.rearrange("b (t p) c -> p (b t) c", p=P), tiles(m.H)).then_inc(stored, 16)
                sp.wait_ge(stored, 16)


def arrays(v):
    g = {k: np.asarray(x) for k, x in v.items()}
    l0, ff = (lambda k: g["L0_attn_" + k]), (lambda k: g["L0_ffn_" + k])
    eye = np.eye(P, dtype=np.float32)
    row = np.arange(P)
    iota = row[:, None].astype(np.float32)
    iota[0] = -1
    table, turns, masks = relative_constants()
    rows, pos = relative_weights(l0("Wq"), l0("bq"), l0("Wk"), l0("bk"), l0("Wpos"), l0("u_bias"), l0("v_bias"))
    zero_row = np.zeros((1, D), np.float32)

    half = 8
    inv = 1.0 / 10000.0 ** (np.arange(0, 16, 2, dtype=np.float32) / 16)
    emb = np.concatenate([np.outer(np.arange(S, dtype=np.float32), inv)] * 2, -1).T
    sign = np.where(np.arange(16) < half, -1, 1)[:, None]
    rope = np.concatenate([np.tile(np.cos(emb), (4, 1)), np.tile(np.sin(emb) * sign, (4, 1))], 1).astype(np.float32)
    causal = []
    for h in range(4):
        q = ff("wq")[16 * h:16 * h + 16].T
        k = ff("wk")[16 * (h // 2):16 * (h // 2) + 16].T
        swap = lambda w: np.concatenate([w[:, half:], w[:, :half]], 1)
        causal.append(np.pad(np.concatenate([q] * 4 + [swap(q)] * 4 + [k] * 4 + [swap(k)] * 4, 1), ((0, 2), (0, 0))))
    zeros22 = np.zeros((D, D - REST), np.float32)
    gated = []
    for e in range(E):
        w1, w3 = ff("w1")[e].T, ff("w3")[e].T
        gated += [w1[:, :P], w3[:, :P], w1[:, P:], zeros22, w3[:, P:]]
    WQ, WK = g["L1_attn_WQ"], g["L1_attn_WK"]
    wide = [np.concatenate([WQ[:, h * D:(h + 1) * D]] * 2 + [WK[:, h * D:(h + 1) * D]] * 2, 1) for h in range(8)]
    e_row = np.arange(E)
    out = dict(
        tokens=g["x"], token_W=g["L0_tok_token_W"], pe_rows=g["L0_tok_pe"][:2].reshape(1, 2 * D), iota=iota,
        ident=eye, split=split_columns(), join32=np.tile(eye[:32, :32], (4, 1)), join64=np.tile(eye[:64, :64], (2, 1)),
        causal_mask=np.where(row[None, :] > row[:, None], NEG, 0).astype(np.float32),
        ln_gamma=l0("ln_gamma"), ln_beta=l0("ln_beta"), rel_v=np.concatenate([l0("Wv"), l0("bv")[None], zero_row]),
        rel_rows=rows, rel_pos=pos, pe_table=table, turns=turns, rel_masks=masks,
        rel_out=np.concatenate([l0("Wout"), l0("bout")[None]]),
        ln1_w=ff("ln1_w"), ln2_w=ff("ln2_w"), causal_qk=np.stack(causal * B), causal_v=ff("wv").T, rope_table=rope,
        causal_out=ff("wo").T, router0=ff("router_w").T, gated_up=np.concatenate(gated, 1),
        gated_down=ff("w2").transpose(2, 0, 1).reshape(HID, E * D),
        before=(e_row[None, :] < e_row[:, None]).astype(np.float32).reshape(E * E),
        wide_qk=np.stack(wide * B), wide_v=g["L1_attn_WV"], wide_out=g["L1_attn_Wout"], wide_bout=g["L1_attn_bout"],
        gamma1=g["L1_ffn_gamma"], beta1=g["L1_ffn_beta"], router1=g["L1_ffn_Wr"], router1_bias=g["L1_ffn_br"],
        gelu_up=g["L1_ffn_W1"].transpose(1, 0, 2).reshape(D, E * P), gelu_b1=g["L1_ffn_b1"].T,
        gelu_down=g["L1_ffn_W2"], gelu_b2=g["L1_ffn_b2"].reshape(1, E * D))
    return {k: np.ascontiguousarray(x) for k, x in out.items()}


def kernel(**inputs):
    import concourse.bacc as bacc
    from concourse.bass_utils import run_bass_kernel_spmd

    nc = bacc.Bacc("TRN2", target_bir_lowering=False, num_devices=1)
    sent, args = {}, {}
    for name, x in arrays(inputs).items():
        sent[name + "_dram"] = x
        args[name] = nc.dram_tensor(name + "_dram", x.shape, mybir.dt.from_np(x.dtype), kind="ExternalInput").ap()
    out = nc.dram_tensor("out_dram", (B, S, D), F32, kind="ExternalOutput").ap()
    tower(nc, args, out)
    result = run_bass_kernel_spmd(nc, [sent], core_ids=[0])
    return result.results[0]["out_dram"]
```

```python
import numpy as np
import concourse.bass as bass
from concourse import mybir
from contextlib import ExitStack

F32 = mybir.dt.float32
F32R = mybir.dt.float32r
I32 = mybir.dt.int32
ALU = mybir.AluOpType
ACT = mybir.ActivationFunctionType
AX = mybir.AxisListType

P = 128
B, S, D = 2, 2048, 64
N = B * S
NT = N // P
TPB = S // P
BANK = 512
VOCAB = 128
SEP_ID, PAD_ID = 13, 1
E = 8
LN_EPS, RMS_EPS = 1e-5, 1e-6
NEG = -1e30


class Machine:

    def __init__(self, nc, whole):
        self.nc, self.whole, self.stage_no, self.sems = nc, whole, 0, []

    def sbuf(self, name, shape, dtype=F32, ctx=None):
        return (ctx or self.whole).enter_context(self.nc.sbuf_tensor(name, shape, dtype))

    def sem(self, name):
        self.sems.append(self.nc.alloc_semaphore(name=name))
        return self.sems[-1]

    def renew_semaphores(self):
        self.nc.clear_and_free_semaphores(self.sems)
        self.nc.all_engine_barrier()
        self.sems = []

    def stage(self, name):
        self.stage_no += 1
        return f"{name}{self.stage_no}"


def bcast(ap, shape, axis):
    return ap.unsqueeze(axis).broadcast_to(shape)


def tiles(t, k=NT):
    return t[:].rearrange("p (t c) -> p t c", t=k)


def embed(m, tokens, token_W, pe_rows, iota):
    nc, tag = m.nc, m.stage("embed")
    with ExitStack() as c:
        ids = m.sbuf("ids", [P, N], I32, c)
        onehot = m.sbuf("onehot", [P, N], F32, c)
        table = m.sbuf("table", [VOCAB, D], F32, c)
        col = m.sbuf("iota_col", [P, 1], F32, c)
        pe01 = m.sbuf("pe01", [1, 2 * D], F32, c)
        is_sep = m.sbuf("is_sep", [1, S], F32, c)
        is_pad = m.sbuf("is_pad", [1, S], F32, c)
        posed = m.sbuf("posed", [1, N], F32, c)
        loaded, hot, mask_step = m.sem(tag + "_loaded"), m.sem(tag + "_hot"), m.sem(tag + "_mask")
        summed, kept = m.sem(tag + "_summed"), m.sem(tag + "_kept")
        block = c.enter_context(nc.Block())
        PER = BANK // D

        @block.sync
        def _(sp):
            sp.dma_start(ids[:], tokens.rearrange("s b -> (s b)").partition_broadcast(P)).then_inc(loaded, 16)
            sp.dma_start(table[:], token_W).then_inc(loaded, 16)
            sp.dma_start(col[:], iota).then_inc(loaded, 16)
            sp.dma_start(pe01[:], pe_rows).then_inc(loaded, 16)

        @block.vector
        def _(dve):
            dve.wait_ge(loaded, 64)
            nc.vector.tensor_scalar(onehot[:], ids[:], col[:, 0:1], None, ALU.is_equal).then_inc(hot, 1)
            nc.vector.memset(posed[0:1, 0:S], 1.0).then_inc(mask_step, 1)
            nc.vector.tensor_scalar(is_sep[:], ids[0:1, 0:S], float(SEP_ID), None, ALU.is_equal).then_inc(mask_step, 1)
            nc.vector.tensor_scalar(is_pad[:], ids[0:1, S:N], float(PAD_ID), None, ALU.is_equal).then_inc(mask_step, 1)
            dve.wait_ge(mask_step, 3)
            nc.vector.tensor_tensor(is_sep[:], is_sep[:], is_pad[:], ALU.mult).then_inc(mask_step, 1)
            dve.wait_ge(mask_step, 4)
            nc.vector.tensor_scalar(posed[0:1, S:N], is_sep[:], -1.0, 1.0, ALU.mult, ALU.add).then_inc(mask_step, 1)
            for g in range(NT // PER):
                dve.wait_ge(summed, g + 1)
                nc.vector.tensor_copy(m.H[:, g * BANK:(g + 1) * BANK], m.bank(g % 2)).then_inc(kept, 1)

        @block.tensor
        def _(pe):
            pe.wait_ge(hot, 1)
            pe.wait_ge(mask_step, 5)
            for t in range(NT):
                g, j = t // PER, t % PER
                if j == 0 and g >= 2:
                    pe.wait_ge(kept, g - 1)
                out = m.bank(g % 2)[:, j * D:(j + 1) * D]
                nc.tensor.matmul(out, onehot[:, t * P:(t + 1) * P], table[:], start=True, stop=False)
                s = t // TPB
                last = nc.tensor.matmul(out, posed[0:1, t * P:(t + 1) * P], pe01[0:1, s * D:(s + 1) * D],
                                        start=False, stop=True)
                if j == PER - 1:
                    last.then_inc(summed, 1)


def normalize(m, src, dst, eps, mean=True, gamma=None, beta=None):
    nc, tag = m.nc, m.stage("norm")
    with ExitStack() as c:
        square = m.sbuf(tag + "_square", [P, NT * D], F32, c)
        stat = m.sbuf(tag + "_stat", [P, 4 * NT], F32, c)
        affine = m.sbuf(tag + "_affine", [P, 2 * D], F32, c)
        eps_col = m.sbuf(tag + "_eps", [P, 1], F32, c)
        sums, means, var, rstd = (stat[:, k * NT:(k + 1) * NT] for k in range(4))
        step, loaded = m.sem(tag + "_step"), m.sem(tag + "_loaded")
        centred, squared, rooted = (m.sem(tag + n) for n in ("_centred", "_squared", "_rooted"))
        block = c.enter_context(nc.Block())
        shape = [P, NT, D]
        loads = [(k, v) for k, v in enumerate((gamma, beta)) if v is not None]

        @block.sync
        def _(sp):
            for k, v in loads:
                sp.dma_start(affine[:, k * D:(k + 1) * D], v.partition_broadcast(P)).then_inc(loaded, 16)

        halves = [slice(k * NT * D // 2, (k + 1) * NT * D // 2) for k in range(2)]
        in_half = lambda t, k: t[:, halves[k]].rearrange("p (t c) -> p t c", c=D)

        @block.scalar
        def _(act):
            for k in range(2):
                if mean:
                    act.wait_ge(centred, k + 1)
                source = dst if mean else src
                nc.scalar.activation(square[:, halves[k]], source[:, halves[k]], ACT.Square).then_inc(squared, 1)
            act.wait_ge(step, 4 if mean else 2)
            nc.scalar.activation(var, var, ACT.Sqrt, bias=eps_col[:, 0:1], scale=1.0 / D).then_inc(rooted, 1)

        @block.vector
        def _(dve):
            n = 0

            def done(instruction):
                nonlocal n
                n += 1
                instruction.then_inc(step, 1)
                dve.wait_ge(step, n)

            if mean:
                done(nc.vector.tensor_reduce(sums, tiles(src), axis=AX.X, op=ALU.add))
                done(nc.vector.tensor_scalar(means, sums, 1.0 / D, None, ALU.mult))
                for k in range(2):
                    nc.vector.tensor_tensor(in_half(dst, k), in_half(src, k),
                                            bcast(means[:, k * NT // 2:(k + 1) * NT // 2], [P, NT // 2, D], 2),
                                            ALU.subtract).then_inc(centred, 1)
            done(nc.vector.memset(eps_col[:], eps))
            for k in range(2):
                dve.wait_ge(squared, k + 1)
                reduced = nc.vector.tensor_reduce(var[:, k * NT // 2:(k + 1) * NT // 2], in_half(square, k),
                                                  axis=AX.X, op=ALU.add)
            done(reduced)
            dve.wait_ge(rooted, 1)
            done(nc.vector.reciprocal(rstd, var))
            done(nc.vector.tensor_tensor(tiles(dst), tiles(dst if mean else src), bcast(rstd, shape, 2), ALU.mult))
            if loads:
                dve.wait_ge(loaded, 16 * len(loads))
            for k, _ in loads:
                done(nc.vector.tensor_tensor(tiles(dst), tiles(dst), bcast(affine[:, k * D:(k + 1) * D], shape, 1),
                                             ALU.mult if k == 0 else ALU.add))


def channels_first(m, src, dst, blocks=1, ones=0):
    nc, tag = m.nc, m.stage("turn")
    turned, copied_v, copied_s = m.sem(tag + "_turned"), m.sem(tag + "_copied_v"), m.sem(tag + "_copied_s")
    PER = BANK // P
    groups = NT // PER
    with ExitStack() as c:
        block = c.enter_context(nc.Block())

        @block.tensor
        def _(pe):
            for g in range(groups):
                if g >= 4:
                    pe.wait_ge(copied_s if g % 2 else copied_v, (g - 4) // 2 + 1)
                for j in range(PER):
                    t = g * PER + j
                    last = nc.tensor.transpose(m.bank(g % 4)[0:D, j * P:(j + 1) * P],
                                               src[:, t * D:(t + 1) * D], m.ident[:])
                last.then_inc(turned, 1)

        @block.vector
        def _(dve):
            for g in range(0, groups, 2):
                dve.wait_ge(turned, g + 1)
                nc.vector.tensor_copy(dst[0:D, g * BANK:(g + 1) * BANK], m.bank(g % 4)[0:D, :]).then_inc(copied_v, 1)

        @block.scalar
        def _(act):
            for g in range(1, groups, 2):
                act.wait_ge(turned, g + 1)
                nc.scalar.activation(dst[0:D, g * BANK:(g + 1) * BANK], m.bank(g % 4)[0:D, :],
                                     ACT.Copy).then_inc(copied_s, 1)

        if ones:
            @block.gpsimd
            def _(pool):
                nc.gpsimd.memset(dst[D:D + ones, :], 1.0)


def project_add(m, ctxT, rows, weight, dst):
    nc, tag = m.nc, m.stage("out")
    PER = BANK // D
    with ExitStack() as c:
        w = m.sbuf(tag + "_w", [rows, D], F32, c)
        loaded, made, added = m.sem(tag + "_loaded"), m.sem(tag + "_made"), m.sem(tag + "_added")
        block = c.enter_context(nc.Block())

        @block.sync
        def _(sp):
            sp.dma_start(w[:], weight).then_inc(loaded, 16)

        @block.tensor
        def _(pe):
            pe.wait_ge(loaded, 16)
            for t in range(NT):
                g, j = t // PER, t % PER
                if j == 0 and g >= 2:
                    pe.wait_ge(added, g - 1)
                last = nc.tensor.matmul(m.bank(g % 2)[:, j * D:(j + 1) * D], ctxT[0:rows, t * P:(t + 1) * P],
                                        w[:], start=True, stop=True)
                if j == PER - 1:
                    last.then_inc(made, 1)

        @block.vector
        def _(dve):
            for g in range(NT // PER):
                dve.wait_ge(made, g + 1)
                nc.vector.tensor_tensor(dst[:, g * BANK:(g + 1) * BANK], m.bank(g % 2),
                                        dst[:, g * BANK:(g + 1) * BANK], ALU.add).then_inc(added, 1)


CHUNK = BANK
CHUNKS = S // CHUNK
QT = CHUNK // P


class Item:

    def __init__(self, kind, c, x=0, y=0, at=0):
        self.kind, self.c, self.x, self.y, self.at = kind, c, x, y, at
        self.n = self.m = self.pair = None


def head_schedule(causal, relative, pairs_at_once):
    keys = lambda c: (c + 1 if causal else CHUNKS) * QT
    pieces = lambda c: [Item("piece", c, t, k) for t in range(QT) for k in range(keys(c) // QT)]

    def order(c):
        near = [k for k in range(QT * c, QT * (c + 1) + 1) if k < keys(c)] if relative else []
        far = [k for k in range(keys(c)) if k not in near]
        n = len(near)
        return [k for pair in zip(near, far) for k in pair] + far[n:]

    last_group = lambda c: Item("values", c, keys(c) // 2 // pairs_at_once - 1)
    first = sorted(pieces(0), key=lambda i: (i.y, i.x))
    items = []
    by_bank = [[i for i in first if i.y == k] for k in range(CHUNKS)]
    if relative:
        b0, b1, b2, b3 = by_bank
        by_bank = [[], [b1[0], b0[0], b1[1], b0[1]], [b1[2], b0[2], b2[0], b1[3], b2[1], b0[3]], b2[2:] + b3]
    if causal:
        by_bank = [first, [Item("rows", 0)], [], []]
    for k in range(CHUNKS + 1):
        items += [Item("prepare", 0, k)] + (by_bank[k - 1] if k else [])
    items += [] if causal else [Item("rows", 0)]
    for c in range(CHUNKS):
        pairs = keys(c) // 2
        ahead = pieces(c + 1) if c + 1 < CHUNKS else []
        if relative:
            ahead.sort(key=lambda i: i.y == i.c or (i.x == QT - 1 and i.y == i.c + 1))
        steps = max(pairs - 2, 1)
        for p in range(pairs):
            step = [Item("score", c, order(c)[at], at=at) for at in (2 * p, 2 * p + 1)]
            if p and p % pairs_at_once == 0:
                step.append(Item("values", c, p // pairs_at_once - 1))
            elif p == 0 and c:
                step.append(last_group(c - 1))
            mine = ahead[len(ahead) * p // steps:len(ahead) * (p + 1) // steps] if p < steps else []
            while step or mine:
                items += mine[:1] + step[:1]
                mine, step = mine[1:], step[1:]
            if p == steps and ahead:
                items.append(Item("rows", c + 1))
            if p == 1 and c:
                items.append(Item("join", c - 1))
    items += [last_group(CHUNKS - 1), Item("join", CHUNKS - 1)]
    count, uses, pair_of = {}, 0, {}
    for i in items:
        i.n = count.get(i.kind, 0)
        count[i.kind] = i.n + 1
        if relative and i.kind == "piece":
            i.diag, i.corner = i.y == i.c, i.x == QT - 1 and i.y == i.c + 1
        elif relative and i.kind == "score":
            i.diag, i.corner = i.x // QT == i.c, i.x == QT * (i.c + 1)
        else:
            i.diag = i.corner = False
        if i.kind in ("rows", "join") or i.diag or i.corner:
            i.m, uses = uses, uses + 1
        if i.kind == "score":
            i.pair = pair_of.setdefault((i.c, i.at // 2), i.n // 2)
        if i.kind == "values":
            i.pair = pair_of[i.c, i.x * pairs_at_once]
            i.last = i.x == keys(i.c) // 2 // pairs_at_once - 1
    return items, count, uses, keys, order


def attention(m, kind, heads, dh, prepare, spare=None):
    nc, tag = m.nc, m.stage(kind)
    causal, relative, wide = kind == "causal", kind == "relative", kind == "wide"
    W = 64 if wide else 32
    groups = P // W
    at_once = groups // 2
    items, count, uses, keys, order = head_schedule(causal, relative, at_once)
    PIECES, PAIRS = count["piece"], count["score"] // 2
    S0, X0, O_BANK, M_BANK = 0, 4, 6, 7
    ROWS_M = P if relative else 66
    row0 = P - 16 if relative else 64
    with ExitStack() as c_:
        probs = [spare[:, k * 2 * BANK:(k + 1) * 2 * BANK] if spare and k < 2 else
                 m.sbuf(f"{tag}_probs{k}", [P, 2 * BANK], F32, c_) for k in range(2 * at_once)]
        outT = [m.sbuf(f"{tag}_outT{k}", [P, CHUNK], F32, c_) for k in range(2)]
        part = [m.sbuf(f"{tag}_part{k}", [P, QT * CHUNKS], F32, c_) for k in range(2)]
        top, recip = m.sbuf(tag + "_top", [P, QT], F32, c_), m.sbuf(tag + "_recip", [P, QT], F32, c_)
        top_hi = m.sbuf(tag + "_top_hi", [P, QT], F32R, c_)
        held = m.sbuf(tag + "_held", [P, 1], F32, c_)
        maxima = m.sbuf(tag + "_maxima", [P, QT * ROWS_M], F32R, c_)
        values = m.sbuf(tag + "_values", [P, TPB * W], F32, c_)
        total = [[m.sbuf(f"{tag}_total{k}{r}", [P, BANK], F32, c_) for r in range(2)] for k in range(2)] if wide else None
        names = ("score_ready piece_ready piece_read small_ready small_read exp_done out_ready outT_done "
                 "maxima_ready row_step recip_step values_in cleared even_sum odd_sum chunk_sum fix_step").split()
        (score_ready, piece_ready, piece_read, small_ready, small_read, exp_done, out_ready, outT_done,
         maxima_ready, row_step, recip_step, values_in, cleared, even_sum, odd_sum, chunk_sum, fix_step) = (
            m.sem(f"{tag}_{n}") for n in names)
        block = c_.enter_context(nc.Block())
        ops = prepare(m, tag, c_)
        small = m.bank(M_BANK)
        ones = m.sbuf(tag + "_ones", [P, 2], F32, c_) if wide else None
        max_cols = maxima[:].rearrange("p (t r) -> p t r", t=QT)
        CLEARED = (2 if wide else 1) + len(ops.constant_rows)
        JW = W + 2 if wide else W
        rows_of = [i for i in items if i.kind == "rows"]
        FIX_STEPS = len([i for i in items if i.diag])
        fixes = [i for i in items if i.kind == "score" and (i.diag or i.corner)]

        @block.sync
        def _(sp):
            ops.load_weights(sp, 0)
            sp.dma_start(values[:], ops.values_of(0)).then_inc(values_in, 16)
            with sp.Fori(1, B * heads) as it:
                sp.wait_ge(ops.weights_used, it * ops.uses)
                ops.load_weights(sp, it)
                sp.wait_ge(small_read, it * uses)
                sp.dma_start(values[:], ops.values_of(it)).then_inc(values_in, 16)

        @block.tensor
        def _(pe):
            pe.wait_ge(cleared, CLEARED)

            def small_free(it, i):
                if i.m:
                    pe.wait_ge(small_read, it * uses + i.m)

            with pe.Fori(0, B) as b, pe.Fori(0, heads) as h:
                it = b * heads + h
                for i in items:
                    if i.kind == "prepare":
                        for k in ([0], [1, 2], [3], [], [])[i.x]:
                            ops.pe_prepare(pe, it, b, k)
                    if i.kind == "piece":
                        if i.n == 0 or i.x == 0 and (i.y == 0 if causal else i.c == 0):
                            ops.piece_ready(pe, it, i.c if causal else i.y)
                        if i.diag or i.corner:
                            small_free(it, i)
                            ops.diagonal_q(i, small).then_inc(small_ready, 1)
                        if i.n >= 2:
                            pe.wait_ge(piece_read, it * PIECES + i.n - 1)
                        ops.piece(i, m.bank(X0 + i.n % 2)).then_inc(piece_ready, 1)
                    if i.kind == "rows":
                        small_free(it, i)
                        pe.wait_ge(maxima_ready, it * CHUNKS + i.c + 1)
                        for t in range(QT):
                            last = nc.tensor.matmul(small[0:ROWS_M, t * P:(t + 1) * P],
                                                    maxima[:, t * ROWS_M:(t + 1) * ROWS_M], m.ident_r[:],
                                                    start=True, stop=True)
                        last.then_inc(small_ready, 1)
                    if i.kind == "score":
                        if i.n == 0:
                            ops.ready(pe, it)
                        if i.at == 0:
                            pe.wait_ge(small_read, it * uses + rows_of[i.c].m + 1)
                        if i.at % 2 == 0 and i.pair >= 2:
                            pe.wait_ge(exp_done, it * PAIRS + i.pair - 1)
                        if i.diag or i.corner:
                            small_free(it, i)
                            ops.diagonal_k(i, small).then_inc(small_ready, 1)
                        ops.score(i, m.bank(S0 + i.pair % 2 * 2 + i.at % 2)).then_inc(score_ready, 1)
                    if i.kind == "values":
                        if i.n == 0:
                            pe.wait_ge(values_in, 16 * (it + 1))
                        pe.wait_ge(exp_done, it * PAIRS + i.pair + at_once)
                        if i.x == 0 and i.c:
                            pe.wait_ge(outT_done, it * CHUNKS + i.c)
                        for g in range(groups):
                            at, tile = groups * i.x + g, probs[(i.pair + g // 2) % (2 * at_once)]
                            last = nc.tensor.matmul(m.bank(O_BANK)[g * W:(g + 1) * W, :],
                                                    values[:, order(i.c)[at] * W:(order(i.c)[at] + 1) * W],
                                                    tile[:, g % 2 * BANK:(g % 2 + 1) * BANK], start=at < groups,
                                                    stop=at >= keys(i.c) - groups, skip_group_check=True)
                        if i.last:
                            last.then_inc(out_ready, 1)
                    if i.kind == "join":
                        small_free(it, i)
                        pe.wait_ge(outT_done, it * CHUNKS + i.c + 1)
                        if wide:
                            pe.wait_ge(chunk_sum, it * CHUNKS + i.c + 1)
                        for t in range(QT):
                            q = slice(t * P, (t + 1) * P)
                            last = nc.tensor.matmul(small[:, t * JW:t * JW + W], outT[i.c % 2][:, q], m.join[W][:],
                                                    start=True, stop=True)
                            if wide:
                                last = nc.tensor.matmul(small[:, t * JW + W:(t + 1) * JW], total[i.c % 2][0][:, q],
                                                        ones[:], start=True, stop=True)
                        last.then_inc(small_ready, 1)
                pe.wait_ge(small_read, (it + 1) * uses)

        @block.scalar
        def _(act):
            with act.Fori(0, B) as b, act.Fori(0, heads) as h:
                it = b * heads + h
                for i in items:
                    if i.kind == "prepare":
                        ops.act_prepare(act, it, i.x)
                    if i.kind == "score" and i.at % 2 == 1:
                        pair = i.pair
                        act.wait_ge(score_ready, (it * PAIRS + pair) * 2 + 2)
                        of_pair = [f for f in fixes if f.pair == pair]
                        if of_pair:
                            act.wait_ge(small_read, it * uses + of_pair[-1].m + 1)
                        if wide and pair >= 2:
                            act.wait_ge(even_sum, it * PAIRS + pair - 1)
                            act.wait_ge(odd_sum, it * PAIRS + pair - 1)
                        nc.scalar.activation(probs[pair % (2 * at_once)][:], m.psum[:, (S0 + pair % 2 * 2) * BANK:
                                                                        (S0 + pair % 2 * 2 + 2) * BANK],
                                             ACT.Exp).then_inc(exp_done, 1)
                    if i.kind == "values" and i.last:
                        act.wait_ge(out_ready, it * CHUNKS + i.c + 1)
                        nc.scalar.activation(outT[i.c % 2][:], m.bank(O_BANK), ACT.Copy).then_inc(outT_done, 1)

        @block.vector
        def _(dve):
            nc.vector.memset(maxima[:].bitcast(F32), 0.0).then_inc(cleared, 1)
            if wide:
                nc.vector.memset(ones[:], 1.0).then_inc(cleared, 1)
            for n, (rows, value) in enumerate(ops.constant_rows):
                nc.vector.memset(rows.bitcast(F32), value).then_inc(cleared, 1)
                dve.wait_ge(cleared, CLEARED - len(ops.constant_rows) + n + 1)
            dve.wait_ge(cleared, CLEARED)
            with dve.Fori(0, B) as b, dve.Fori(0, heads) as h:
                it = b * heads + h
                steps = 0
                for i in items:
                    if i.kind == "prepare":
                        ops.dve_prepare(dve, it, i.x)
                    if i.kind == "piece":
                        bank = m.bank(X0 + i.n % 2)
                        dve.wait_ge(piece_ready, it * PIECES + i.n + 1)
                        if i.diag or i.corner:
                            dve.wait_ge(small_ready, it * uses + i.m + 1)
                            steps += replace(dve, ops.fixes_q(i, bank, small), held, small_read, fix_step,
                                             it * FIX_STEPS + steps)
                            dve.wait_ge(small_read, it * uses + i.m + 1)
                        nc.vector.tensor_reduce(part[i.c % 2][:, i.x * CHUNKS + i.y:i.x * CHUNKS + i.y + 1],
                                                bank[:, 0:(i.x + 1) * P] if causal and i.y == i.c else bank,
                                                axis=AX.X, op=ALU.max).then_inc(piece_read, 1)
                    if i.kind == "score" and (i.diag or i.corner):
                        bank = m.bank(S0 + i.pair % 2 * 2 + i.at % 2)
                        dve.wait_ge(score_ready, it * PAIRS * 2 + i.n + 1)
                        dve.wait_ge(small_ready, it * uses + i.m + 1)
                        steps += replace(dve, ops.fixes_k(i, bank, small), held, small_read, fix_step,
                                         it * FIX_STEPS + steps)
                        dve.wait_ge(small_read, it * uses + i.m + 1)
                    if i.kind == "values" and wide:
                        acc, half = total[i.c % 2][1][:], probs[i.pair % (2 * at_once)][:, BANK:]
                        dve.wait_ge(exp_done, it * PAIRS + i.pair + 1)
                        if i.x:
                            dve.wait_ge(odd_sum, it * PAIRS + i.pair)
                            nc.vector.tensor_tensor(acc, acc, half, ALU.add).then_inc(odd_sum, 1)
                        else:
                            nc.vector.tensor_copy(acc, half).then_inc(odd_sum, 1)
                    if i.kind == "rows":
                        banks = keys(i.c) // QT
                        n0 = (it * CHUNKS + i.c) * 3
                        dve.wait_ge(piece_read, it * PIECES + len([j for j in items if j.kind == "piece" and j.c <= i.c]))
                        nc.vector.tensor_reduce(top[:], part[i.c % 2][:].rearrange("p (t k) -> p t k", t=QT)[:, :, 0:banks],
                                                axis=AX.X, op=ALU.max, negate=True).then_inc(row_step, 1)
                        dve.wait_ge(row_step, n0 + 1)
                        nc.vector.tensor_copy(top_hi[:], top[:]).then_inc(row_step, 1)
                        dve.wait_ge(row_step, n0 + 2)
                        nc.vector.tensor_copy(max_cols[:, :, row0], top_hi[:].bitcast(F32)).then_inc(row_step, 1)
                        nc.vector.tensor_tensor(max_cols[:, :, row0 + 1], top[:], top_hi[:].bitcast(F32),
                                                ALU.subtract).then_inc(maxima_ready, 1)
                        dve.wait_ge(small_ready, it * uses + i.m + 1)
                        last = ops.place_rows(i.c, small)
                        last.then_inc(small_read, 1)
                    if i.kind == "join":
                        made = small[:, 0:QT * JW].rearrange("p (t w) -> p t w", t=QT)
                        dve.wait_ge(small_ready, it * uses + i.m + 1)
                        nc.vector.reciprocal(recip[:], made[:, :, dh]).then_inc(recip_step, 1)
                        dve.wait_ge(recip_step, it * CHUNKS + i.c + 1)
                        nc.vector.tensor_tensor(ops.context(b, h, i.c), made[:, :, 0:dh],
                                                bcast(recip[:], [P, QT, dh], 2), ALU.mult).then_inc(small_read, 1)

        @block.gpsimd
        def _(pool):
            with pool.Fori(0, B) as b, pool.Fori(0, heads) as h:
                it = b * heads + h
                for k in range(CHUNKS + 1):
                    ops.pool_prepare(pool, it, k)
                if wide:
                    for i in items:
                        if i.kind == "values":
                            acc, half = total[i.c % 2][0][:], probs[i.pair % (2 * at_once)][:, 0:BANK]
                            pool.wait_ge(exp_done, it * PAIRS + i.pair + 1)
                            if i.x:
                                pool.wait_ge(even_sum, it * PAIRS + i.pair)
                            nc.gpsimd.tensor_tensor(acc, half, acc if i.x else m.split[:, 7:8].broadcast_to([P, BANK]),
                                                    ALU.add if i.x else ALU.mult).then_inc(even_sum, 1)
                            if i.last:
                                pool.wait_ge(even_sum, it * PAIRS + i.pair + 1)
                                pool.wait_ge(odd_sum, it * PAIRS + i.pair + 1)
                                nc.gpsimd.tensor_tensor(acc, acc, total[i.c % 2][1][:], ALU.add).then_inc(chunk_sum, 1)


def replace(dve, fixes, held, small_read, step, before):
    for n, (scores, mask, data) in enumerate(fixes):
        dve.memset(held[:], 0.0)
        last = n == len(fixes) - 1
        dve.copy_predicated(scores, mask, data).then_inc(small_read if last else step, 1)
        if not last:
            dve.wait_ge(step, before + n + 1)
    return len(fixes) - 1


class Operands:
    pass


def split_columns():
    row = np.arange(P)
    lo_q, lo_k, lo_w = (row // 32) % 2, (row // 16) % 2, row // 64
    lo_k3 = (row // 16) % 4 == 1
    cols = [lo_q / 8, 1 - 2 * lo_q, 1 * lo_k3, 1 - 2 * lo_k3, lo_w, 1 - 2 * lo_w, lo_q / 4, 0 * row + 1]
    upper = row < 64
    cols += [np.where(upper, 1 / 4, 1), np.where(upper, lo_q / 4, lo_k), np.where(upper, 1 - 2 * lo_q, 1 - 2 * lo_k)]
    return np.stack(cols, 1).astype(np.float32)


def all_values(m, XT, rows, weight, kind, Vall):
    nc, tag = m.nc, m.stage("values")
    wide = kind == "wide"
    cols = weight.shape[1]
    W, heads = (64, 8) if wide else (32, 4)
    per = BANK // cols
    V = Vall[:].rearrange("p (b h t w) -> p b h t w", b=B, h=heads, t=TPB)
    with ExitStack() as c:
        w = m.sbuf(tag + "_w", [rows, cols], F32, c)
        loaded, made, kept, cleared = (m.sem(tag + x) for x in ("_loaded", "_made", "_kept", "_cleared"))
        block = c.enter_context(nc.Block())

        @block.sync
        def _(sp):
            sp.dma_start(w[:], weight).then_inc(loaded, 16)

        @block.gpsimd
        def _(pool):
            if not wide:
                nc.gpsimd.memset(Vall[:], 0.0).then_inc(cleared, 1)
                pool.wait_ge(cleared, 1)
                nc.gpsimd.memset(Vall[:].rearrange("p (n w) -> p n w", w=W)[:, :, 16:17], 1.0).then_inc(cleared, 1)

        @block.tensor
        def _(pe):
            pe.wait_ge(loaded, 16)
            for t in range(NT):
                g, j = t // per, t % per
                if j == 0 and g >= 2:
                    pe.wait_ge(kept, g - 1)
                last = nc.tensor.matmul(m.bank(g % 2)[:, j * cols:(j + 1) * cols], XT[0:rows, t * P:(t + 1) * P],
                                        w[:], start=True, stop=True)
                if j == per - 1:
                    last.then_inc(made, 1)

        @block.vector
        def _(dve):
            if not wide:
                dve.wait_ge(cleared, 2)
            for g in range(NT // per):
                dve.wait_ge(made, g + 1)
                b, t = g * per // TPB, g * per % TPB
                if wide:
                    nc.vector.tensor_copy(V[:, b, :, t, :],
                                          m.bank(g % 2).rearrange("p (h d) -> p h d", h=heads)).then_inc(kept, 1)
                    continue
                kv = cols // 16
                for j in range(per):
                    made_kv = m.bank(g % 2)[:, j * cols:(j + 1) * cols].rearrange("p (h d) -> p h d", h=kv)
                    for r in range(heads // kv):
                        out = V[:, b, r::heads // kv, t + j, 0:16]
                        last = nc.vector.tensor_copy(out, made_kv)
                last.then_inc(kept, 1)


def relative_tables(m, pe_dup, KA, KB, QAu, QBu):
    nc, tag = m.nc, m.stage("tables")
    with ExitStack() as c:
        full = m.sbuf(tag + "_pe", [P, S], F32, c)
        loaded, rounded_hi = m.sem(tag + "_loaded"), m.sem(tag + "_rounded_hi")
        block = c.enter_context(nc.Block())

        @block.sync
        def _(sp):
            sp.dma_start(full[:], pe_dup).then_inc(loaded, 16)

        @block.vector
        def _(dve):
            dve.wait_ge(loaded, 16)
            nc.vector.tensor_copy(KA[0:64, :], full[0:64, :]).then_inc(rounded_hi, 1)
            nc.vector.tensor_copy(KB[64:P, :], full[64:P, :])
            dve.wait_ge(rounded_hi, 1)
            nc.vector.tensor_tensor(KB[0:64, :], full[0:64, :], KA[0:64, :].bitcast(F32), ALU.subtract)
            nc.vector.memset(QAu[:, S:S + 2].bitcast(F32), 0.0)
            nc.vector.memset(QBu[:, S:S + 2].bitcast(F32), 0.0)


def relative_operands(XS, Vall, w_content, w_bias, w_pos, KA, KB, QAl, QBl, QAu, QBu, turn, masks, ctx_out):
    def prepare(m, tag, c):
        nc = m.nc
        COLS = 2 * P
        full, bias = (m.sbuf(tag + n, [P, COLS], F32, c) for n in ("_w", "_bias"))
        hi, lo, bias_r = (m.sbuf(tag + n, [P, COLS], F32R, c) for n in ("_w_hi", "_w_lo", "_bias_r"))
        wp = m.sbuf(tag + "_wp", [16, 2 * P + COLS], F32, c)
        comb, comb_r = m.sbuf(tag + "_comb", [P, 2 * COLS], F32, c), m.sbuf(tag + "_comb_r", [P, 2 * COLS], F32R, c)
        comb_lo = m.sbuf(tag + "_comb_lo", [P, COLS], F32R, c)
        ones, ones_f = m.sbuf(tag + "_ones_r", [P, BANK], F32R, c), m.split[:, 7:8].broadcast_to([P, COLS])
        bias_lo = slice(32, 64)
        products = [m.sbuf(f"{tag}_products{k}", [P, 4 * BANK], F32, c) for k in range(2)]
        hi_part = [m.sbuf(f"{tag}_hi{k}", [P, 2 * BANK], F32R, c) for k in range(2)]
        x_part = [m.sbuf(f"{tag}_x{k}", [P, 2 * BANK], F32, c) for k in range(2)]
        weights_in, weights_split, comb_ready, comb_raised, comb_done, made_content = (m.sem(tag + x) for x in (
            "_weights_in", "_weights_split", "_comb_ready", "_comb_raised", "_comb_done", "_made_content"))
        made, halved, multiplied, content, turned_q, highs, lows, shifted = (
            m.sem(tag + x) for x in ("_made", "_halved", "_multiplied", "_content", "_turned_q", "_highs", "_lows", "_shifted"))
        NC = S // BANK
        UP = P - 2
        ops = Operands()
        low = slice(64, P)
        forms = ((QAl, QBl), (QAu, QBu))

        def load_weights(sp, it):
            for tile, source in ((full[0:D, :], w_content), (full[D:P, :], w_content), (bias[:], w_bias), (wp[:], w_pos)):
                sp.dma_start(tile, source[bass.ds(it, 1)].rearrange("a k m -> (a k) m")).then_inc(weights_in, 16)

        def product(out, w_hi, w_lo, w_bias_r, tokens):
            nc.tensor.matmul(out, w_hi, tokens, start=True, stop=False)
            nc.tensor.matmul(out, w_lo, tokens, start=False, stop=False)
            return nc.tensor.matmul(out, w_bias_r, ones[:], start=False, stop=True)

        def pe_prepare(pe, it, b, k):
            if k == 0:
                pe.wait_ge(weights_in, 64 * (it + 1))
                for n in range(2):
                    last = nc.tensor.matmul(m.bank(7)[:, n * COLS:(n + 1) * COLS], wp[:, n * P:(n + 1) * P],
                                            wp[:, 2 * P:], start=True, stop=True)
                last.then_inc(comb_ready, 1)
                pe.wait_ge(weights_split, 4 * (it + 1))
            else:
                pe.wait_ge(halved, (it * NC + k) * 4)
            tokens = XS[:, bass.ds(b * S + k * BANK, BANK)]
            for n in range(2):
                cols = slice(n * P, (n + 1) * P)
                last = product(m.bank(2 + n), hi[:, cols], lo[:, cols], bias_r[:, cols], tokens)
            last.then_inc(made_content, 1)
            if k == 0:
                pe.wait_ge(comb_raised, 2 * (it + 1))
                pe.wait_ge(comb_done, 2 * (it + 1))
            else:
                pe.wait_ge(multiplied, (it * NC + k) * 4)
            for n in range(2):
                cols = slice(n * P, (n + 1) * P)
                last = product(m.bank(n), comb_r[:, cols], comb_lo[:, cols],
                               comb_r[:, COLS + n * P:COLS + (n + 1) * P], tokens)
            last.then_inc(made, 1)

        def piece_ready(pe, it, y):
            pe.wait_ge(content, (it * NC + y + 1) * 2)
            pe.wait_ge(shifted, it * NC + 1)
            pe.wait_ge(highs, (it * NC + 2) * 4)

        def ready(pe, it):
            pe.wait_ge(shifted, (it + 1) * NC)
            pe.wait_ge(lows, (it + 1) * NC * 2)

        def act_prepare(act, it, step):
            k = step
            if k == 0:
                act.wait_ge(comb_ready, it + 1)
                for out in (comb, comb_r):
                    nc.scalar.activation(out[:], m.bank(7), ACT.Copy, scale=1 / 8).then_inc(comb_raised, 1)
            if k < NC:
                act.wait_ge(made_content, it * NC + k + 1)
                if k >= 2:
                    act.wait_ge(content, (it * NC + k - 1) * 2)
                bank = m.psum[low, 2 * BANK:4 * BANK]
                for n in range(2):
                    part = slice(n * BANK, (n + 1) * BANK)
                    nc.scalar.activation(hi_part[k % 2][low, part], bank[:, part], ACT.Copy,
                                         scale=1 / 8 if n == 0 else 1.0).then_inc(halved, 1)
                    nc.scalar.activation(x_part[k % 2][low, part], bank[:, part], ACT.Copy,
                                         scale=m.split[low, 2 * n:2 * n + 1]).then_inc(halved, 1)
            k = step - 1
            if k >= 0:
                cols = slice(k * BANK, (k + 1) * BANK)
                act.wait_ge(turned_q, (it * NC + k + 1) * 2)
                for n, (QA, QB) in enumerate(forms):
                    turned = products[k % 2][:, n * 2 * BANK:(n * 2 + 1) * BANK]
                    nc.scalar.activation(QB[:, cols], turned, ACT.Copy).then_inc(highs, 1)
                    nc.scalar.activation(QA[0:64, cols], turned[0:64, :], ACT.Copy).then_inc(highs, 1)

        def dve_prepare(dve, it, step):
            k = step
            if k == 0:
                dve.wait_ge(comb_raised, 2 * (it + 1))
                nc.vector.tensor_tensor(comb_lo[:], comb[:, 0:COLS], comb_r[:, 0:COLS].bitcast(F32),
                                        ALU.subtract).then_inc(comb_done, 1)
                nc.vector.tensor_tensor(comb_r[bias_lo, COLS:], comb[bias_lo, COLS:], comb_r[bias_lo, COLS:].bitcast(F32),
                                        ALU.subtract).then_inc(comb_done, 1)
            if k < NC:
                cols = slice(k * BANK, (k + 1) * BANK)
                dve.wait_ge(made, it * NC + k + 1)
                if k >= 2:
                    dve.wait_ge(lows, (it * NC + k - 1) * 2)
                for n in range(4):
                    nc.vector.tensor_tensor(products[k % 2][:, n * BANK:(n + 1) * BANK], m.bank(n % 2),
                                            turn[:, n * S + k * BANK:n * S + (k + 1) * BANK],
                                            ALU.mult).then_inc(multiplied, 1)
                dve.wait_ge(halved, (it * NC + k + 1) * 4)
                for out, n in ((QAl, 0), (KA, 1)):
                    part = slice(n * BANK, (n + 1) * BANK)
                    nc.vector.scalar_tensor_tensor(out[low, cols], hi_part[k % 2][low, part].bitcast(F32),
                                                   m.split[low, 2 * n + 1:2 * n + 2], x_part[k % 2][low, part],
                                                   ALU.mult, ALU.add).then_inc(content, 1)
            k = step - 1
            if k >= 0:
                cols = slice(k * BANK, (k + 1) * BANK)
                dve.wait_ge(highs, (it * NC + k + 1) * 4)
                for n, (QA, QB) in enumerate(forms):
                    nc.vector.tensor_tensor(QB[low, cols], products[k % 2][low, n * 2 * BANK:(n * 2 + 1) * BANK],
                                            QB[low, cols].bitcast(F32), ALU.subtract).then_inc(lows, 1)

        def pool_prepare(pool, it, k):
            if k == 0:
                pool.wait_ge(weights_in, 64 * (it + 1))
                nc.gpsimd.tensor_tensor(hi[:], full[:], ones_f, ALU.mult).then_inc(weights_split, 1)
                nc.gpsimd.tensor_tensor(bias_r[:], bias[:], ones_f, ALU.mult).then_inc(weights_split, 1)
                pool.wait_ge(weights_split, 4 * it + 2)
                nc.gpsimd.tensor_tensor(lo[:], full[:], hi[:].bitcast(F32), ALU.subtract).then_inc(weights_split, 1)
                pool.wait_ge(weights_split, 4 * it + 3)
                nc.gpsimd.tensor_tensor(bias_r[bias_lo, :], bias[bias_lo, :], bias_r[bias_lo, :].bitcast(F32),
                                        ALU.subtract).then_inc(weights_split, 1)
                pool.wait_ge(weights_split, 4 * it + 4)
            if k < NC:
                pool.wait_ge(multiplied, (it * NC + k + 1) * 4)
                for n in range(2):
                    first, second = (products[k % 2][:, (n * 2 + r) * BANK:(n * 2 + r + 1) * BANK] for r in range(2))
                    nc.gpsimd.tensor_tensor(first, first, second, ALU.add).then_inc(turned_q, 1)
                pool.wait_ge(turned_q, (it * NC + k + 1) * 2)
                pool.wait_ge(content, (it * NC + k) * 2 + 1)
                nc.gpsimd.tensor_tensor(QAu[low, k * BANK + 1:(k + 1) * BANK + 1],
                                        QAl[low, k * BANK:(k + 1) * BANK].bitcast(F32),
                                        m.split[low, 7:8].broadcast_to([64, BANK]), ALU.mult).then_inc(shifted, 1)
                pool.wait_ge(shifted, it * NC + k + 1)

        def two(out, keys, QA, QB, queries):
            nc.tensor.matmul(out, KA[:, keys], QA[:, queries], start=True, stop=False)
            return nc.tensor.matmul(out, KB[:, keys], QB[:, queries], start=False, stop=True)

        def piece(i, bank):
            q, first = (i.c * QT + i.x) * P, i.y * BANK
            edge = min(max(q + P, first), first + BANK) - first
            if edge:
                last = nc.tensor.matmul(bank[:, 0:edge], QAl[:, q:q + P], KA[:, first:first + edge], start=True, stop=True)
            if edge < BANK:
                last = nc.tensor.matmul(bank[:, edge:], QAu[:, q + 1:q + 1 + P], KA[:, first + edge:first + BANK],
                                        start=True, stop=True)
            return last

        def beyond(i):
            return 0 if i.x == QT - 1 else 2

        def diagonal_q(i, small):
            q = (i.c * QT + i.x) * P
            if i.corner:
                return nc.tensor.matmul(small[:, 0:2], QAl[low, q:q + P], KA[low, q + P:q + P + 2], start=True, stop=True)
            nc.tensor.matmul(small[:, 0:UP], QAu[:, q + 1:q + 1 + P], KA[:, q + 2:q + P], start=True, stop=True)
            n = P + beyond(i)
            return nc.tensor.matmul(small[:, UP:UP + n], QAl[low, q:q + P], KA[low, q:q + n], start=True, stop=True)

        def fixes_q(i, bank, small):
            q, n = i.x * P, P + beyond(i)
            if i.corner:
                return ((bank[:, 0:2], masks[:, 2 * P:2 * P + 2], small[:, 0:2]),)
            return ((bank[:, q + 2:q + P], masks[:, 2:P], small[:, 0:UP]),
                    (bank[:, q:q + n], masks[:, P:P + n], small[:, UP:UP + n]))

        def score(i, bank):
            q = i.c * CHUNK
            edge = min(max(i.x * P - q, 0), CHUNK)
            keys = slice(i.x * P, (i.x + 1) * P)
            if edge:
                last = two(bank[:, 0:edge], keys, QAu, QBu, slice(q + 1, q + 1 + edge))
            if edge < CHUNK:
                last = two(bank[:, edge:], keys, QAl, QBl, slice(q + edge, q + CHUNK))
            return last

        def before(i):
            return 0 if i.x % QT == 0 else 2

        def diagonal_k(i, small):
            keys, q = slice(i.x * P, (i.x + 1) * P), i.x * P
            if i.corner:
                return nc.tensor.matmul(small[:, 0:2], KA[low, keys], QAl[low, q - 2:q], start=True, stop=True)
            two(small[:, 0:UP], keys, QAu, QBu, slice(q + 1, q + 1 + UP))
            n = before(i)
            return nc.tensor.matmul(small[:, UP:UP + P + n], KA[low, keys], QAl[low, q - n:q + P], start=True, stop=True)

        def fixes_k(i, bank, small):
            q, n, at = i.x % QT * P, before(i), 2 * P + 2
            if i.corner:
                return ((bank[:, CHUNK - 2:], masks[:, at + P:at + P + 2], small[:, 0:2]),)
            return ((bank[:, q:q + UP], masks[:, at:at + UP], small[:, 0:UP]),
                    (bank[:, q - n:q + P], masks[:, at + P + 2 - n:at + 2 * P + 2], small[:, UP:UP + P + n]))

        def place_rows(n, small):
            rows = slice(96, P)
            for first, QA in ((n * CHUNK, QAl), (n * CHUNK + 1, QAu)):
                own = QA[rows, first:first + CHUNK]
                last = nc.vector.tensor_tensor(own, own.bitcast(F32), small[rows, :], ALU.add)
            return last

        ops.constant_rows = ((ones[:], 1.0),)
        ops.weights_used, ops.uses = made, NC
        ops.load_weights, ops.pe_prepare, ops.act_prepare = load_weights, pe_prepare, act_prepare
        ops.dve_prepare, ops.pool_prepare = dve_prepare, pool_prepare
        ops.piece, ops.score, ops.place_rows = piece, score, place_rows
        ops.piece_ready, ops.ready = piece_ready, ready
        ops.diagonal_q, ops.diagonal_k, ops.fixes_q, ops.fixes_k = diagonal_q, diagonal_k, fixes_q, fixes_k
        ops.values_of = lambda it: Vall[:, bass.ds(it * (TPB * 32), TPB * 32)]
        ops.context = lambda b, h, n: ctx_out[:].rearrange("p (t c) -> p t c", t=NT)[
            :, bass.ds(b * TPB + n * QT, QT), bass.ds(h * 16, 16)]
        return ops
    return prepare


def relative_constants():
    freq = np.exp(np.arange(0, D, 2, dtype=np.float32) * np.float32(-np.log(10000.0) / D)).astype(np.float64)
    t = np.arange(S, dtype=np.float64)
    angle = np.repeat(freq, 2)[:, None]
    even = (np.arange(D) % 2 == 0)[:, None]
    table = np.where(even, np.sin(angle * t), np.cos(angle * t))
    turns = []
    for a in (S - 1 - t, -(t + 1)):
        turns += [np.cos(angle * a), np.where(even, -np.sin(angle * a), np.sin(angle * a))]
    twice = lambda x: np.concatenate([x, x], 0).astype(np.float32)
    i, j = np.arange(P)[:, None], np.arange(P + 2)[None, :]
    masks = np.concatenate([j[:, :P] > i + 1, j == i + 1, i > j[:, :P] + 1, i == j - 1], 1).astype(np.int32)
    return twice(table), np.concatenate([twice(x) for x in turns], 1), masks


def swap_pairs(w):
    return w.reshape(*w.shape[:-1], -1, 2)[..., ::-1].reshape(w.shape)


def relative_weights(Wq, bq, Wk, bk, Wpos, u, v):
    rows, biases, pos = [], [], []
    none = np.zeros((D, 16), np.float32)
    for h in range(4):
        s = slice(16 * h, 16 * h + 16)
        zero = np.zeros((D, D), np.float32)
        rows.append(np.concatenate([zero] + [Wq[:, s]] * 3 + [none, zero] + [Wk[:, s]] * 3 + [none], 1))
        bias = np.zeros((P, 2, P), np.float32)
        pq = np.zeros((16, 2, P), np.float32)
        pq[:, 0] = np.concatenate([Wq[:, s]] * 2, 0).T
        for first in (0, 32):
            for copy in range(3):
                cols = slice(D + 16 * copy, D + 16 * copy + 16)
                bias[first, 0, cols], bias[first + 1, 0, cols], bias[first, 1, cols] = bq[s], u[h], bk[s]
            pq[:, 1, first], pq[:, 1, first + 1] = bq[s], v[h]
        bias[0, 1, D + 48:D + 50] = 1
        biases.append(bias.reshape(P, 2 * P))
        p = Wpos[:, s].T
        sw = swap_pairs(p)
        pos.append(np.concatenate([pq.reshape(16, 2 * P), p, p, sw, sw], 1))
    return np.stack(rows * B), np.stack(biases * B), np.stack(pos * B)


class HeadWeights:

    def __init__(self, m, tag, source, cols, c):
        self.nc, self.source = m.nc, source
        self.full = m.sbuf(tag + "_w", [P, cols], F32, c)
        self.hi, self.lo = (m.sbuf(tag + n, [P, cols], F32R, c) for n in ("_w_hi", "_w_lo"))
        self.one = m.split[:, 7:8].broadcast_to([P, cols])
        self.loaded, self.ready = m.sem(tag + "_w_loaded"), m.sem(tag + "_w_ready")

    def load(self, sp, it):
        for rows in (slice(0, D), slice(D, P)):
            sp.dma_start(self.full[rows, :],
                         self.source[bass.ds(it, 1)].rearrange("a k m -> (a k) m")).then_inc(self.loaded, 16)

    def split(self, pool, it):
        pool.wait_ge(self.loaded, 32 * (it + 1))
        self.nc.gpsimd.tensor_tensor(self.hi[:], self.full[:], self.one, ALU.mult).then_inc(self.ready, 1)
        pool.wait_ge(self.ready, 2 * it + 1)
        self.nc.gpsimd.tensor_tensor(self.lo[:], self.full[:], self.hi[:].bitcast(F32), ALU.subtract).then_inc(self.ready, 1)

    def wait(self, pe, it):
        pe.wait_ge(self.ready, 2 * (it + 1))

    def product(self, out, n, tokens):
        cols = slice(n * P, (n + 1) * P)
        self.nc.tensor.matmul(out, self.hi[:, cols], tokens, start=True, stop=False)
        return self.nc.tensor.matmul(out, self.lo[:, cols], tokens, start=False, stop=True)


def rounded(m, pairs):
    nc = m.nc
    with nc.Block() as block:
        @block.vector
        def _(dve):
            for out, source in pairs:
                nc.vector.tensor_copy(out, source)


def causal_operands(XS, Vall, weights, rope, ident, mask, ctx_out):
    def prepare(m, tag, c):
        nc = m.nc
        weights_of = HeadWeights(m, tag, weights, 4 * D, c)
        products = [m.sbuf(f"{tag}_products{k}", [P, 2 * BANK], F32, c) for k in range(2)]
        hi_part = [m.sbuf(f"{tag}_hi{k}", [P, BANK], F32R, c) for k in range(2)]
        x_part = [m.sbuf(f"{tag}_x{k}", [P, BANK], F32, c) for k in range(2)]
        QS, KS = (m.sbuf(tag + n, [P, S], F32R, c) for n in ("_QS", "_KS"))
        made, halved, multiplied, content, summed = (
            m.sem(tag + x) for x in ("_made", "_halved", "_multiplied", "_content", "_summed"))
        NC = S // BANK
        ops = Operands()

        def pe_prepare(pe, it, b, k):
            if k == 0:
                weights_of.wait(pe, it)
            if k >= 2:
                pe.wait_ge(multiplied, (it * NC + k - 1) * 2)
            for n in range(2):
                last = weights_of.product(m.bank(k % 2 * 2 + n), n, XS[:, bass.ds(b * S + k * BANK, BANK)])
            last.then_inc(made, 1)

        def piece_ready(pe, it, n):
            pe.wait_ge(content, (it * NC + n + 1) * 2)

        def ready(pe, it):
            pe.wait_ge(multiplied, (it + 1) * NC * 2)

        def dve_prepare(dve, it, step):
            k = step
            if k < NC:
                dve.wait_ge(made, it * NC + k + 1)
                if k >= 2:
                    dve.wait_ge(halved, (it * NC + k - 1) * 2)
                for n in range(2):
                    nc.vector.tensor_tensor(products[k % 2][:, n * BANK:(n + 1) * BANK],
                                            m.bank(k % 2 * 2 + n),
                                            rope[:, n * S + k * BANK:n * S + (k + 1) * BANK],
                                            ALU.mult).then_inc(multiplied, 1)
            k = step - 1
            if k >= 0:
                cols = slice(k * BANK, (k + 1) * BANK)
                dve.wait_ge(halved, (it * NC + k + 1) * 2)
                for rows, out in ((slice(0, D), QS), (slice(D, P), KS)):
                    nc.vector.scalar_tensor_tensor(out[0:D, cols], hi_part[k % 2][rows, :].bitcast(F32),
                                                   m.split[rows, 10:11], x_part[k % 2][rows, :], ALU.mult,
                                                   ALU.add).then_inc(content, 1)

        def pool_prepare(pool, it, k):
            if k == 0:
                weights_of.split(pool, it)
            if k < NC:
                pool.wait_ge(multiplied, (it * NC + k + 1) * 2)
                first, second = (products[k % 2][:, r * BANK:(r + 1) * BANK] for r in range(2))
                nc.gpsimd.tensor_tensor(first, first, second, ALU.add).then_inc(summed, 1)

        def act_prepare(act, it, k):
            if k < NC:
                act.wait_ge(summed, it * NC + k + 1)
                if k >= 2:
                    act.wait_ge(content, (it * NC + k - 1) * 2)
                for out, factor in ((hi_part, 8), (x_part, 9)):
                    nc.scalar.activation(out[k % 2][:], products[k % 2][:, 0:BANK], ACT.Copy,
                                         scale=m.split[:, factor:factor + 1]).then_inc(halved, 1)

        def piece(i, bank):
            q, keys = (i.c * QT + i.x) * P, i.y * BANK
            n = (i.x + 1) * P if i.y == i.c else BANK
            last = nc.tensor.matmul(bank[:, 0:n], QS[0:D, q:q + P], KS[0:D, keys:keys + n], start=True,
                                    stop=i.y != i.c)
            if i.y == i.c:
                last = nc.tensor.matmul(bank[:, n - P:n], ident[:], mask[:, BANK:], start=False, stop=True)
            return last

        def score(i, bank):
            r, q = i.x - i.c * QT, slice(i.c * CHUNK, (i.c + 1) * CHUNK)
            last = nc.tensor.matmul(bank, KS[:, i.x * P:(i.x + 1) * P], QS[:, q], start=True, stop=r < 0)
            if r >= 0:
                last = nc.tensor.matmul(bank[:, 0:(r + 1) * P], ident[:], mask[:, BANK - (r + 1) * P:BANK],
                                        start=False, stop=True)
            return last

        def place_rows(n, small):
            return nc.vector.tensor_copy(QS[D:D + 2, n * CHUNK:(n + 1) * CHUNK], small[D:D + 2, :])

        ops.constant_rows = ((KS[D:P, :], 0.0), (KS[D:D + 2, :], 1.0), (QS[D:P, :], 0.0))
        ops.weights_used, ops.uses = made, NC
        ops.load_weights, ops.pe_prepare, ops.act_prepare = weights_of.load, pe_prepare, act_prepare
        ops.dve_prepare, ops.pool_prepare = dve_prepare, pool_prepare
        ops.piece, ops.score, ops.place_rows = piece, score, place_rows
        ops.piece_ready, ops.ready = piece_ready, ready
        ops.values_of = lambda it: Vall[:, bass.ds(it * (TPB * 32), TPB * 32)]
        ops.context = lambda b, h, n: ctx_out[:].rearrange("p (t c) -> p t c", t=NT)[
            :, bass.ds(b * TPB + n * QT, QT), bass.ds(h * 16, 16)]
        return ops
    return prepare


def wide_values(m, XS, w_hi, w_lo, values_dram):
    nc, tag = m.nc, m.stage("values")
    cols, PER = 8 * D, 4
    groups = NT // PER
    with ExitStack() as c:
        staged = [m.sbuf(f"{tag}_staged{k}", [P, PER * cols], F32, c) for k in range(2)]
        made, kept_v, kept_s = (m.sem(tag + x) for x in ("_made", "_kept_v", "_kept_s"))
        stored = [m.sem(f"{tag}_stored{k}") for k in range(2)]
        block = c.enter_context(nc.Block())

        def copied_to(g, j):
            return staged[g % 2][:].rearrange("p (h t d) -> p h t d", h=8, t=PER)[:, :, j, :]

        @block.sync
        def _(sp):
            for g in range(groups):
                sp.wait_ge(kept_v, 2 * (g + 1))
                sp.wait_ge(kept_s, 2 * (g + 1))
                b, t = g * PER // TPB, g * PER % TPB
                sp.dma_start(values_dram[b * 8:(b + 1) * 8, :, t * D:(t + PER) * D].rearrange("h p n -> p h n"),
                             staged[g % 2][:].rearrange("p (h n) -> p h n", h=8)).then_inc(stored[g % 2], 16)
            for k in range(2):
                sp.wait_ge(stored[k], 16 * (groups // 2))

        @block.tensor
        def _(pe):
            for t in range(NT):
                if t >= 4:
                    pe.wait_ge(kept_s if t % 2 else kept_v, (t - 4) // 2 + 1)
                nc.tensor.matmul(m.bank(t % 4), XS[:, t * P:(t + 1) * P], w_hi[:], start=True, stop=False)
                nc.tensor.matmul(m.bank(t % 4), XS[:, t * P:(t + 1) * P], w_lo[:], start=False, stop=True).then_inc(made, 1)

        @block.vector
        def _(dve):
            for t in range(0, NT, 2):
                dve.wait_ge(made, t + 1)
                g, j = t // PER, t % PER
                if g >= 2 and j == 0:
                    dve.wait_ge(stored[g % 2], 16 * (g // 2))
                nc.vector.tensor_copy(copied_to(g, j), m.bank(t % 4).rearrange("p (h d) -> p h d", h=8)).then_inc(kept_v, 1)

        @block.scalar
        def _(act):
            for t in range(1, NT, 2):
                act.wait_ge(made, t + 1)
                g, j = t // PER, t % PER
                if g >= 2 and j == 1:
                    act.wait_ge(stored[g % 2], 16 * (g // 2))
                nc.scalar.activation(copied_to(g, j), m.bank(t % 4).rearrange("p (h d) -> p h d", h=8),
                                     ACT.Copy).then_inc(kept_s, 1)


def wide_operands(XS, values_dram, weights, ctx_out):
    def prepare(m, tag, c):
        nc = m.nc
        weights_of = HeadWeights(m, tag, weights, 4 * D, c)
        scaled = [m.sbuf(f"{tag}_scaled{k}", [D, BANK], F32, c) for k in range(2)]
        QH, KS = (m.sbuf(tag + n, [P, S], F32R, c) for n in ("_QH", "_KS"))
        QL, KB = (m.sbuf(tag + n, [P, S], F32R, c) for n in ("_QL", "_KB"))
        made, queries, keys_hi, keys_done, lows = (
            m.sem(tag + x) for x in ("_made", "_queries", "_keys_hi", "_keys_done", "_lows"))
        NC = S // BANK
        scale = float(np.float32(1) / np.float32(np.sqrt(8)))
        ops = Operands()

        def pe_prepare(pe, it, b, k):
            if k == 0:
                weights_of.wait(pe, it)
            if k >= 2:
                pe.wait_ge(keys_done, it * NC + k - 1)
                pe.wait_ge(queries, it * NC + k - 1)
            for n in range(2):
                last = weights_of.product(m.bank(k % 2 * 2 + n), n, XS[:, bass.ds(b * S + k * BANK, BANK)])
            last.then_inc(made, 1)

        def piece_ready(pe, it, y):
            pe.wait_ge(keys_done, it * NC + y + 1)
            if y == 0:
                pe.wait_ge(queries, it * NC + 1)

        def ready(pe, it):
            pe.wait_ge(queries, (it + 1) * NC)
            pe.wait_ge(lows, (it + 1) * NC * 2)

        def act_prepare(act, it, k):
            if k < NC:
                cols, bank = slice(k * BANK, (k + 1) * BANK), k % 2 * 2
                act.wait_ge(made, it * NC + k + 1)
                nc.scalar.activation(KS[:, cols], m.bank(bank + 1), ACT.Copy).then_inc(keys_hi, 1)
                if k >= 2:
                    act.wait_ge(lows, (it * NC + k - 1) * 2)
                nc.scalar.activation(scaled[k % 2][:], m.bank(bank)[0:D, :], ACT.Copy, scale=scale)
                nc.scalar.activation(QH[:, cols], m.bank(bank), ACT.Copy, scale=scale).then_inc(queries, 1)

        def dve_prepare(dve, it, k):
            if k < NC:
                cols = slice(k * BANK, (k + 1) * BANK)
                dve.wait_ge(keys_hi, it * NC + k + 1)
                nc.vector.tensor_tensor(KS[D:P, cols], m.bank(k % 2 * 2 + 1)[D:P, :], KS[D:P, cols].bitcast(F32),
                                        ALU.subtract).then_inc(keys_done, 1)

        def pool_prepare(pool, it, k):
            if k == 0:
                weights_of.split(pool, it)
                pool.wait_ge(weights_of.ready, 2 * (it + 1))
            if k < NC:
                cols = slice(k * BANK, (k + 1) * BANK)
                pool.wait_ge(queries, it * NC + k + 1)
                nc.gpsimd.tensor_tensor(QL[0:D, cols], scaled[k % 2][:], QH[0:D, cols].bitcast(F32),
                                        ALU.subtract).then_inc(lows, 1)
                nc.gpsimd.tensor_tensor(KB[0:D, cols], KS[0:D, cols].bitcast(F32),
                                        m.split[0:D, 7:8].broadcast_to([D, BANK]), ALU.mult).then_inc(lows, 1)

        def piece(i, bank):
            q = (i.c * QT + i.x) * P
            return nc.tensor.matmul(bank, QH[:, q:q + P], KS[:, i.y * BANK:(i.y + 1) * BANK], start=True, stop=True)

        def score(i, bank):
            q, k = slice(i.c * CHUNK, (i.c + 1) * CHUNK), slice(i.x * P, (i.x + 1) * P)
            nc.tensor.matmul(bank, KS[:, k], QH[:, q], start=True, stop=False)
            return nc.tensor.matmul(bank, KB[:, k], QL[:, q], start=False, stop=True)

        def place_rows(n, small):
            return nc.vector.tensor_copy(QL[D:D + 2, n * CHUNK:(n + 1) * CHUNK], small[D:D + 2, :])

        ops.constant_rows = ((KB[D:P, :], 0.0), (KB[D:D + 2, :], 1.0), (QL[D:P, :], 0.0))
        ops.weights_used, ops.uses = made, NC
        ops.load_weights, ops.pe_prepare, ops.act_prepare = weights_of.load, pe_prepare, act_prepare
        ops.dve_prepare, ops.pool_prepare = dve_prepare, pool_prepare
        ops.piece, ops.score, ops.place_rows = piece, score, place_rows
        ops.piece_ready, ops.ready = piece_ready, ready
        ops.values_of = lambda it: values_dram[bass.ds(it, 1)].rearrange("a p n -> (a p) n")
        ops.context = lambda b, h, n: ctx_out[:].rearrange("p (t c) -> p t c", t=NT)[
            :, bass.ds(b * TPB + n * QT, QT), bass.ds(h * D, D)]
        return ops
    return prepare


def project_wide(m, ctx, weight, bias, dst):
    nc, tag = m.nc, m.stage("outw")
    PIECES = 8 * D // P
    with ExitStack() as c:
        w = m.sbuf(tag + "_w", [P, PIECES * D], F32, c)
        b_all = m.sbuf(tag + "_bias", [P, D], F32, c)
        turnedT = [m.sbuf(f"{tag}_ctxT{k}", [P, PIECES * P], F32, c) for k in range(2)]
        loaded, turned, copied, made, added, biased = (
            m.sem(tag + x) for x in ("_loaded", "_turned", "_copied", "_made", "_added", "_biased"))
        block = c.enter_context(nc.Block())

        @block.sync
        def _(sp):
            sp.dma_start(w[:].rearrange("p (q d) -> p q d", q=PIECES),
                         weight.rearrange("(q p) d -> p q d", p=P)).then_inc(loaded, 16)
            sp.dma_start(b_all[:], bias.partition_broadcast(P)).then_inc(loaded, 16)

        @block.tensor
        def _(pe):
            pe.wait_ge(loaded, 32)
            for step in range(NT + 1):
                if step < NT:
                    if step >= 2:
                        pe.wait_ge(copied, step - 1)
                    for q in range(PIECES):
                        last = nc.tensor.transpose(m.bank(step % 2)[:, q * P:(q + 1) * P],
                                                   ctx[:, (step * PIECES + q) * P:(step * PIECES + q + 1) * P],
                                                   m.ident[:])
                    last.then_inc(turned, 1)
                t = step - 1
                if t >= 0:
                    pe.wait_ge(copied, t + 1)
                    if t >= 2:
                        pe.wait_ge(added, t - 1)
                    for q in range(PIECES):
                        last = nc.tensor.matmul(m.bank(2 + t % 2)[:, 0:D], turnedT[t % 2][:, q * P:(q + 1) * P],
                                                w[:, q * D:(q + 1) * D], start=q == 0, stop=q == PIECES - 1)
                    last.then_inc(made, 1)

        @block.scalar
        def _(act):
            for t in range(NT):
                act.wait_ge(turned, t + 1)
                if t >= 2:
                    act.wait_ge(made, t - 1)
                nc.scalar.activation(turnedT[t % 2][:], m.bank(t % 2), ACT.Copy).then_inc(copied, 1)

        @block.vector
        def _(dve):
            dve.wait_ge(loaded, 32)
            nc.vector.tensor_tensor(tiles(dst), tiles(dst), bcast(b_all[:], [P, NT, D], 1), ALU.add).then_inc(biased, 1)
            dve.wait_ge(biased, 1)
            for t in range(NT):
                dve.wait_ge(made, t + 1)
                nc.vector.tensor_tensor(dst[:, t * D:(t + 1) * D], m.bank(2 + t % 2)[:, 0:D],
                                        dst[:, t * D:(t + 1) * D], ALU.add).then_inc(added, 1)


def split_channels(m, src, FS):
    nc, tag = m.nc, m.stage("split")
    PER = BANK // P
    groups = NT // PER
    with ExitStack() as c:
        hi = [m.sbuf(f"{tag}_hi{k}", [P, BANK], F32R, c) for k in range(2)]
        x = [m.sbuf(f"{tag}_x{k}", [P, BANK], F32, c) for k in range(2)]
        twice = m.sbuf(tag + "_twice", [P, 2 * NT * D], F32, c)
        doubled_p, doubled_s, turned, halved, scaled, joined = (
            m.sem(tag + n) for n in ("_doubled_p", "_doubled_s", "_turned", "_halved", "_scaled", "_joined"))
        block = c.enter_context(nc.Block())

        def doubling(g):
            out = twice[:, g * 2 * PER * D:(g + 1) * 2 * PER * D].rearrange("p (t r d) -> p t r d", t=PER, r=2)
            one = src[:, g * PER * D:(g + 1) * PER * D].rearrange("p (t d) -> p t d", t=PER)
            return out, bcast(one, [P, PER, 2, D], 2)

        @block.gpsimd
        def _(pool):
            for g in range(0, groups, 2):
                out, one = doubling(g)
                nc.gpsimd.tensor_copy(out, one).then_inc(doubled_p, 1)

        @block.tensor
        def _(pe):
            for g in range(groups):
                pe.wait_ge(doubled_s if g % 2 else doubled_p, g // 2 + 1)
                if g >= 2:
                    pe.wait_ge(halved, g - 1)
                    pe.wait_ge(scaled, g - 1)
                for j in range(PER):
                    t = g * PER + j
                    last = nc.tensor.transpose(m.bank(g % 2)[:, j * P:(j + 1) * P],
                                               twice[:, t * 2 * D:(t + 1) * 2 * D], m.ident[:])
                last.then_inc(turned, 1)

        @block.scalar
        def _(act):
            for g in range(groups):
                if g % 2 == 0:
                    out, one = doubling(g + 1)
                    nc.scalar.activation(out, one, ACT.Copy).then_inc(doubled_s, 1)
                act.wait_ge(turned, g + 1)
                if g >= 2:
                    act.wait_ge(joined, g - 1)
                nc.scalar.activation(hi[g % 2][:], m.bank(g % 2), ACT.Copy).then_inc(halved, 1)

        @block.vector
        def _(dve):
            for g in range(groups):
                dve.wait_ge(halved, g + 1)
                if g >= 2:
                    dve.wait_ge(joined, g - 1)
                nc.vector.tensor_scalar(x[g % 2][:], m.bank(g % 2), m.split[:, 4:5], None, ALU.mult).then_inc(scaled, 1)
                dve.wait_ge(scaled, g + 1)
                nc.vector.scalar_tensor_tensor(FS[:, g * BANK:(g + 1) * BANK], hi[g % 2][:].bitcast(F32),
                                               m.split[:, 5:6], x[g % 2][:], ALU.mult, ALU.add).then_inc(joined, 1)


def split_weights(m, source, hi, lo):
    nc, tag = m.nc, m.stage("wsplit")
    with ExitStack() as c:
        full = m.sbuf(tag + "_full", [P, hi.shape[1]], F32, c)
        loaded, step = m.sem(tag + "_loaded"), m.sem(tag + "_step")
        block = c.enter_context(nc.Block())

        @block.sync
        def _(sp):
            sp.dma_start(full[0:D, :], source).then_inc(loaded, 16)
            sp.dma_start(full[D:P, :], source).then_inc(loaded, 16)

        @block.vector
        def _(dve):
            dve.wait_ge(loaded, 32)
            nc.vector.tensor_copy(hi[:], full[:]).then_inc(step, 1)
            dve.wait_ge(step, 1)
            nc.vector.tensor_tensor(lo[:], full[:], hi[:].bitcast(F32), ALU.subtract).then_inc(step, 1)


def route(m, FS, r_hi, r_lo, bias, before, gates):
    nc, tag = m.nc, m.stage("route")
    probs_first = bias is None
    with ExitStack() as c:
        logits, expo = (m.sbuf(tag + n, [P, NT * E], F32, c) for n in ("_logits", "_expo"))
        more, same = (m.sbuf(tag + n, [P, NT * E * E], F32, c) for n in ("_more", "_same"))
        rank = m.sbuf(tag + "_rank", [P, NT * E], F32, c)
        stat = m.sbuf(tag + "_stat", [P, 2 * NT], F32, c)
        order = m.sbuf(tag + "_order", [P, E * E + E], F32, c)
        loaded, made, step, raised = (m.sem(tag + n) for n in ("_loaded", "_made", "_step", "_raised"))
        block = c.enter_context(nc.Block())
        top, total = stat[:, 0:NT], stat[:, NT:2 * NT]
        by_e = lambda t: t[:].rearrange("p (t e) -> p t e", e=E)
        pairs = lambda t: t[:].rearrange("p (t e f) -> p t e f", e=E, f=E)
        shape, shape4 = [P, NT, E], [P, NT, E, E]

        @block.sync
        def _(sp):
            sp.dma_start(order[:, 0:E * E], before.partition_broadcast(P)).then_inc(loaded, 16)
            if bias is not None:
                sp.dma_start(order[:, E * E:], bias.partition_broadcast(P)).then_inc(loaded, 16)

        @block.tensor
        def _(pe):
            for t in range(NT):
                out = m.bank(0)[:, t * E:(t + 1) * E]
                nc.tensor.matmul(out, FS[:, t * P:(t + 1) * P], r_hi, start=True, stop=False)
                last = nc.tensor.matmul(out, FS[:, t * P:(t + 1) * P], r_lo, start=False, stop=True)
            last.then_inc(made, 1)

        @block.scalar
        def _(act):
            act.wait_ge(step, 3)
            nc.scalar.activation(expo[:], expo[:], ACT.Exp).then_inc(raised, 1)

        @block.vector
        def _(dve):
            n = 0

            def done(instruction):
                nonlocal n
                n += 1
                instruction.then_inc(step, 1)
                dve.wait_ge(step, n)

            dve.wait_ge(made, 1)
            dve.wait_ge(loaded, 16 if probs_first else 32)
            if probs_first:
                done(nc.vector.tensor_copy(logits[:], m.bank(0)[:, 0:NT * E]))
            else:
                done(nc.vector.tensor_tensor(by_e(logits), m.bank(0)[:, 0:NT * E].rearrange("p (t e) -> p t e", e=E),
                                             bcast(order[:, E * E:], shape, 1), ALU.add))
            done(nc.vector.tensor_reduce(top, by_e(logits), axis=AX.X, op=ALU.max))
            done(nc.vector.tensor_tensor(by_e(expo), by_e(logits), bcast(top, shape, 2), ALU.subtract))
            dve.wait_ge(raised, 1)
            ranked = logits
            if probs_first:
                done(nc.vector.tensor_reduce(total, by_e(expo), axis=AX.X, op=ALU.add))
                done(nc.vector.reciprocal(total, total))
                done(nc.vector.tensor_tensor(by_e(expo), by_e(expo), bcast(total, shape, 2), ALU.mult))
                ranked = expo
            others, own = bcast(by_e(ranked), shape4, 2), bcast(by_e(ranked), shape4, 3)
            done(nc.vector.tensor_tensor(pairs(more), others, own, ALU.is_gt))
            done(nc.vector.tensor_tensor(pairs(same), others, own, ALU.is_equal))
            flat = lambda t: t[:].rearrange("p (t n) -> p t n", t=NT)
            done(nc.vector.tensor_tensor(flat(same), flat(same), bcast(order[:, 0:E * E], [P, NT, E * E], 1), ALU.mult))
            done(nc.vector.tensor_tensor(more[:], more[:], same[:], ALU.add))
            done(nc.vector.tensor_reduce(by_e(rank), pairs(more), axis=AX.X, op=ALU.add))
            done(nc.vector.tensor_scalar(rank[:], rank[:], 1.5, None, ALU.is_lt))
            done(nc.vector.tensor_tensor(expo[:], expo[:], rank[:], ALU.mult))
            done(nc.vector.tensor_reduce(total, by_e(expo), axis=AX.X, op=ALU.add))
            if probs_first:
                done(nc.vector.tensor_scalar(total, total, 1e-9, None, ALU.add))
            done(nc.vector.reciprocal(total, total))
            done(nc.vector.tensor_tensor(by_e(gates), by_e(expo), bcast(total, shape, 2), ALU.mult))


HID = int(8 / 3 * D)
REST = HID - P
GATED_COLS = 2 * P + D + REST


def mix_gated(m, FS, w_hi, w_lo, down, gates, dst):
    nc, tag = m.nc, m.stage("gated")
    CH = 2 * P
    with ExitStack() as c:
        hidden = [m.sbuf(f"{tag}_hidden{k}", [P, 2 * CH], F32, c) for k in range(2)]
        act_part = [m.sbuf(f"{tag}_act{k}", [P, 2 * CH], F32, c) for k in range(2)]
        w_down = m.sbuf(tag + "_down", [P, 2 * E * D], F32, c)
        weighted = m.sbuf(tag + "_weighted", [P, E * D], F32, c)
        summed = m.sbuf(tag + "_summed", [P, D], F32, c)
        loaded, cleared, made, silu, ready, used, out_read, mix_step = (
            m.sem(tag + n) for n in "_loaded _cleared _made _silu _ready _used _out_read _mix_step".split())
        block = c.enter_context(nc.Block())
        NCH = N // CH
        view = lambda t: t[:].rearrange("p (e d) -> p e d", e=E)

        @block.sync
        def _(sp):
            sp.dma_start(w_down[:, 0:E * D], down[0:P, :]).then_inc(loaded, 16)
            sp.wait_ge(cleared, 3)
            sp.dma_start(w_down[0:REST, E * D:], down[P:HID, :]).then_inc(loaded, 16)

        @block.gpsimd
        def _(pool):
            nc.gpsimd.memset(w_down[:, E * D:], 0.0).then_inc(cleared, 1)
            for tile in hidden:
                nc.gpsimd.memset(tile[:, CH:], 0.0).then_inc(cleared, 1)

        @block.tensor
        def _(pe):
            pe.wait_ge(loaded, 32)
            with pe.Fori(0, NCH // 2) as pair:
                for step in range(2 * E + 1):
                    s = step
                    if s < 2 * E:
                        e, k = s % E, s % 2
                        if s >= 2:
                            pe.wait_ge(ready, (pair * 2 * E + s - 1) * 2)
                        tokens = bass.ds((pair * 2 + s // E) * CH, CH)
                        base = e * GATED_COLS
                        for out, lo, wid in ((m.bank(2 * k)[:, 0:CH], 0, P), (m.bank(2 * k)[:, CH:], P, P),
                                             (m.bank(2 * k + 1)[0:D + REST, 0:CH], 2 * P, D + REST)):
                            nc.tensor.matmul(out, w_hi[:, base + lo:base + lo + wid], FS[:, tokens], start=True, stop=False)
                            last = nc.tensor.matmul(out, w_lo[:, base + lo:base + lo + wid], FS[:, tokens],
                                                    start=False, stop=True)
                        last.then_inc(made, 1)
                    s = step - 1
                    if s >= 0:
                        e, k = s % E, s % 2
                        pe.wait_ge(ready, (pair * 2 * E + s + 1) * 2)
                        if e == 0:
                            pe.wait_ge(out_read, OUT_FREE + (pair * 2 + s // E - 1) * 2)
                        for t in range(2):
                            out = m.bank(4 + s // E * 2 + t)[:, e * D:(e + 1) * D]
                            nc.tensor.matmul(out, hidden[k][:, t * P:(t + 1) * P], w_down[:, e * D:(e + 1) * D],
                                             start=True, stop=False)
                            last = nc.tensor.matmul(out, hidden[k][:, CH + t * P:CH + (t + 1) * P],
                                                    w_down[:, (E + e) * D:(E + e + 1) * D], start=False, stop=True)
                        last.then_inc(used, 1)

        @block.scalar
        def _(act):
            with act.Fori(0, NCH // 2) as pair:
                for s in range(2 * E):
                    k = s % 2
                    act.wait_ge(made, pair * 2 * E + s + 1)
                    if s >= 2:
                        act.wait_ge(ready, (pair * 2 * E + s - 1) * 2)
                    nc.scalar.activation(act_part[k][:, 0:CH], m.bank(2 * k)[:, 0:CH], ACT.Silu).then_inc(silu, 1)
                    nc.scalar.activation(act_part[k][0:REST, CH:], m.bank(2 * k + 1)[0:REST, 0:CH],
                                         ACT.Silu).then_inc(silu, 1)

        @block.vector
        def _(dve):
            nc.vector.memset(weighted[:], 0.0).then_inc(out_read, OUT_FREE)
            dve.wait_ge(out_read, OUT_FREE)
            dve.wait_ge(cleared, 3)
            with dve.Fori(0, NCH // 2) as pair:
                for s in range(2 * E):
                    k, at = s % 2, (pair * 2 * E + s) * 2
                    if s >= 2:
                        dve.wait_ge(used, pair * 2 * E + s - 1)
                    dve.wait_ge(silu, at + 1)
                    nc.vector.tensor_tensor(hidden[k][:, 0:CH], act_part[k][:, 0:CH], m.bank(2 * k)[:, CH:],
                                            ALU.mult).then_inc(ready, 1)
                    dve.wait_ge(silu, at + 2)
                    nc.vector.tensor_tensor(hidden[k][0:REST, CH:], act_part[k][0:REST, CH:],
                                            m.bank(2 * k + 1)[D:D + REST, 0:CH], ALU.mult).then_inc(ready, 1)
                    if s in (E + 1, E + 3):
                        mix_outputs(m, dve, pair * 2, (s - E) // 2, 4, gates, weighted, summed, dst, out_read, mix_step)
                dve.wait_ge(used, (pair + 1) * 2 * E)
                for t in range(2):
                    mix_outputs(m, dve, pair * 2 + 1, t, 6, gates, weighted, summed, dst, out_read, mix_step)


OUT_FREE = 4


def mix_outputs(m, dve, n, t, bank0, gates, weighted, summed, dst, out_read, mix_step, b2=None):
    nc = m.nc
    view = lambda t: t.rearrange("p (e d) -> p e d", e=E)
    STEPS = 2 if b2 is None else 3
    steps = (n * 2 + t) * STEPS
    gate = bcast(gates[:, bass.ds((n * 2 + t) * E, E)], [P, E, D], 2)
    if b2 is None:
        nc.vector.tensor_tensor(view(weighted[:]), view(m.bank(bank0 + t)), gate, ALU.mult).then_inc(out_read, 1)
    else:
        nc.vector.tensor_tensor(weighted[:], m.bank(bank0 + t), b2[:], ALU.add).then_inc(out_read, 1)
    dve.wait_ge(out_read, OUT_FREE + n * 2 + t + 1)
    if b2 is not None:
        nc.vector.tensor_tensor(view(weighted[:]), view(weighted[:]), gate, ALU.mult).then_inc(mix_step, 1)
        dve.wait_ge(mix_step, steps + 1)
    nc.vector.tensor_reduce(summed[:], weighted[:].rearrange("p (e d) -> p d e", e=E), axis=AX.X,
                            op=ALU.add).then_inc(mix_step, 1)
    dve.wait_ge(mix_step, steps + STEPS - 1)
    own = dst[:, bass.ds((n * 2 + t) * D, D)]
    nc.vector.tensor_tensor(own, own, summed[:], ALU.add).then_inc(mix_step, 1)
    dve.wait_ge(mix_step, steps + STEPS)


def mix_gelu(m, FS, w_hi, w_lo, b1, down, b2, gates, dst):
    nc, tag = m.nc, m.stage("gelu")
    CH = 2 * P
    with ExitStack() as c:
        hidden = [m.sbuf(f"{tag}_hidden{k}", [P, CH], F32, c) for k in range(2)]
        w_down = m.sbuf(tag + "_down", [P, E * D], F32, c)
        b1_col = m.sbuf(tag + "_b1", [P, E], F32, c)
        b2_all = m.sbuf(tag + "_b2", [P, E * D], F32, c)
        weighted = m.sbuf(tag + "_weighted", [P, E * D], F32, c)
        summed = m.sbuf(tag + "_summed", [P, D], F32, c)
        loaded, made, raised, used, out_read, mix_step = (
            m.sem(tag + n) for n in "_loaded _made _raised _used _out_read _mix_step".split())
        block = c.enter_context(nc.Block())
        NCH = N // CH

        @block.sync
        def _(sp):
            sp.dma_start(w_down[:].rearrange("p (e d) -> p e d", e=E), down.rearrange("e h d -> h e d")).then_inc(loaded, 16)
            sp.dma_start(b1_col[:], b1).then_inc(loaded, 16)
            sp.dma_start(b2_all[:], b2.partition_broadcast(P)).then_inc(loaded, 16)

        @block.tensor
        def _(pe):
            pe.wait_ge(loaded, 48)
            with pe.Fori(0, NCH // 2) as pair:
                for step in range(2 * E + 1):
                    s = step
                    if s < 2 * E:
                        e = s % E
                        if s >= 2:
                            pe.wait_ge(raised, pair * 2 * E + s - 1)
                        out, tokens = m.bank(s % 2)[:, 0:CH], bass.ds((pair * 2 + s // E) * CH, CH)
                        nc.tensor.matmul(out, w_hi[:, e * P:(e + 1) * P], FS[:, tokens], start=True, stop=False)
                        nc.tensor.matmul(out, w_lo[:, e * P:(e + 1) * P], FS[:, tokens], start=False,
                                         stop=True).then_inc(made, 1)
                    s = step - 1
                    if s >= 0:
                        e = s % E
                        pe.wait_ge(raised, pair * 2 * E + s + 1)
                        if e == 0:
                            pe.wait_ge(out_read, OUT_FREE + (pair * 2 + s // E - 1) * 2)
                        for t in range(2):
                            last = nc.tensor.matmul(m.bank(4 + s // E * 2 + t)[:, e * D:(e + 1) * D],
                                                    hidden[s % 2][:, t * P:(t + 1) * P], w_down[:, e * D:(e + 1) * D],
                                                    start=True, stop=True)
                        last.then_inc(used, 1)

        @block.scalar
        def _(act):
            act.wait_ge(loaded, 48)
            with act.Fori(0, NCH // 2) as pair:
                for s in range(2 * E):
                    act.wait_ge(made, pair * 2 * E + s + 1)
                    if s >= 2:
                        act.wait_ge(used, pair * 2 * E + s - 1)
                    nc.scalar.activation(hidden[s % 2][:], m.bank(s % 2)[:, 0:CH], ACT.Gelu,
                                         bias=b1_col[:, s % E:s % E + 1]).then_inc(raised, 1)

        @block.vector
        def _(dve):
            dve.wait_ge(loaded, 48)
            nc.vector.memset(weighted[:], 0.0).then_inc(out_read, OUT_FREE)
            dve.wait_ge(out_read, OUT_FREE)
            with dve.Fori(0, NCH // 2) as pair:
                for half in range(2):
                    dve.wait_ge(used, (pair * 2 + half + 1) * E)
                    for t in range(2):
                        mix_outputs(m, dve, pair * 2 + half, t, 4 + 2 * half, gates, weighted, summed, dst, out_read,
                                    mix_step, b2_all)


def add(m, dst, src):
    nc, half = m.nc, NT * D // 2
    with nc.Block() as block:
        @block.vector
        def _(dve):
            nc.vector.tensor_tensor(dst[:, 0:half], dst[:, 0:half], src[:, 0:half], ALU.add)

        @block.gpsimd
        def _(pool):
            nc.gpsimd.tensor_tensor(dst[:, half:], dst[:, half:], src[:, half:], ALU.add)


def load(m, pairs):
    nc, loaded = m.nc, m.sem(m.stage("load"))
    with nc.Block() as block:
        @block.sync
        def _(sp):
            for sb, dram in pairs:
                sp.dma_start(sb, dram).then_inc(loaded, 16)
            sp.wait_ge(loaded, 16 * len(pairs))


def tower(nc, a, out):
    whole = ExitStack()
    with whole:
        m = Machine(nc, whole)
        m.psum = whole.enter_context(nc.psum_tensor("psum", [P, 8 * BANK], F32))
        m.bank = lambda k: m.psum[:, k * BANK:(k + 1) * BANK]
        m.H = m.sbuf("H", [P, NT * D])
        m.ident, m.split = m.sbuf("ident_sb", [P, P]), m.sbuf("split_sb", [P, 11])
        m.join = {w: m.sbuf(f"join{w}_sb", [P, w]) for w in (32, 64)}
        m.ident_r = m.sbuf("ident_r", [P, P], F32R)
        X, Y = m.sbuf("X", [P, NT * D]), m.sbuf("Y", [P, NT * D])
        load(m, [(m.ident[:], a["ident"]), (m.split[:], a["split"]), (m.join[32][:], a["join32"]),
                 (m.join[64][:], a["join64"])])
        rounded(m, [(m.ident_r[:], m.ident[:])])
        embed(m, a["tokens"], a["token_W"], a["pe_rows"], a["iota"])

        normalize(m, m.H, X, LN_EPS)
        normalize(m, X, X, LN_EPS, gamma=a["ln_gamma"], beta=a["ln_beta"])
        with ExitStack() as c:
            Vall = m.sbuf("Vall0", [P, B * 4 * TPB * 32], F32, c)
            with ExitStack() as c2:
                XT = m.sbuf("XT0", [D + 2, N], F32, c2)
                channels_first(m, X, XT, ones=2)
                all_values(m, XT, D + 2, a["rel_v"], "relative", Vall)
            XS = m.sbuf("XS0", [P, N], F32R, c)
            split_channels(m, X, XS)
            with ExitStack() as c2:
                KA, KB, QAl, QBl = (m.sbuf(n, [P, S], F32R, c2) for n in ("KA", "KB", "QAl", "QBl"))
                QAu, QBu = (m.sbuf(n, [P, S + 2], F32R, c2) for n in ("QAu", "QBu"))
                turn, masks = m.sbuf("turn", [P, 4 * S], F32, c2), m.sbuf("masks", [P, 4 * P + 4], I32, c2)
                load(m, [(turn[:], a["turns"]), (masks[:], a["rel_masks"])])
                relative_tables(m, a["pe_table"], KA, KB, QAu, QBu)
                attention(m, "relative", 4, 16, relative_operands(
                    XS, Vall, a["rel_rows"], a["rel_bias"], a["rel_pos"], KA, KB, QAl, QBl, QAu, QBu, turn, masks, Y), X)
            XT = m.sbuf("CT0", [D + 1, N], F32, c)
            channels_first(m, Y, XT, ones=1)
            project_add(m, XT, D + 1, a["rel_out"], m.H)

        m.renew_semaphores()

        normalize(m, m.H, X, LN_EPS)
        normalize(m, X, Y, RMS_EPS, mean=False, gamma=a["ln1_w"])
        with ExitStack() as c:
            XT = m.sbuf("XT1", [D, N], F32, c)
            channels_first(m, Y, XT)
            XS = m.sbuf("XS1", [P, N], F32R, c)
            split_channels(m, Y, XS)
            Vall = m.sbuf("Vall1", [P, B * 4 * TPB * 32], F32, c)
            all_values(m, XT, D, a["causal_v"], "causal", Vall)
            rope = m.sbuf("rope", [P, 2 * S], F32, c)
            mask, mask_r = (m.sbuf(n, [P, BANK + P], t, c) for n, t in (("mask", F32), ("mask_r", F32R)))
            load(m, [(rope[:], a["rope_table"]), (mask[:], a["causal_mask"])])
            rounded(m, [(mask_r[:], mask[:])])
            attention(m, "causal", 4, 16, causal_operands(XS, Vall, a["causal_qk"], rope, m.ident_r, mask_r, Y))
            channels_first(m, Y, XT)
            project_add(m, XT, D, a["causal_out"], X)
        normalize(m, X, Y, RMS_EPS, mean=False, gamma=a["ln2_w"])
        add(m, m.H, X)
        with ExitStack() as c:
            FS = m.sbuf("FS0", [P, N], F32R, c)
            split_channels(m, Y, FS)
            cols = E * GATED_COLS
            w_hi, w_lo = (m.sbuf(n, [P, cols], F32R, c) for n in ("gated_hi", "gated_lo"))
            r_hi, r_lo = (m.sbuf(n, [P, E], F32R, c) for n in ("router0_hi", "router0_lo"))
            split_weights(m, a["gated_up"], w_hi, w_lo)
            split_weights(m, a["router0"], r_hi, r_lo)
            gates = m.sbuf("gates0", [P, NT * E], F32, c)
            route(m, FS, r_hi[:], r_lo[:], None, a["before"], gates)
            mix_gated(m, FS, w_hi, w_lo, a["gated_down"], gates, m.H)

        m.renew_semaphores()

        normalize(m, m.H, X, LN_EPS)
        with ExitStack() as c:
            CTX = m.sbuf("CTX", [P, NT * 8 * D], F32, c)
            with ExitStack() as c2:
                XS = m.sbuf("XS2", [P, N], F32R, c2)
                split_channels(m, X, XS)
                values = nc.dram_tensor("wide_values", [B * 8, P, TPB * D], F32).ap()
                with ExitStack() as c3:
                    v_hi, v_lo = (m.sbuf(n, [P, 8 * D], F32R, c3) for n in ("wide_v_hi", "wide_v_lo"))
                    split_weights(m, a["wide_v"], v_hi, v_lo)
                    wide_values(m, XS, v_hi, v_lo, values)
                attention(m, "wide", 8, D, wide_operands(XS, values, a["wide_qk"], CTX))
            project_wide(m, CTX, a["wide_out"], a["wide_bout"], m.H)

        normalize(m, m.H, X, LN_EPS)
        normalize(m, X, X, LN_EPS, gamma=a["gamma1"], beta=a["beta1"])
        with ExitStack() as c:
            FS = m.sbuf("FS1", [P, N], F32R, c)
            split_channels(m, X, FS)
            w_hi, w_lo = (m.sbuf(n, [P, E * P], F32R, c) for n in ("gelu_hi", "gelu_lo"))
            r_hi, r_lo = (m.sbuf(n, [P, E], F32R, c) for n in ("router1_hi", "router1_lo"))
            split_weights(m, a["gelu_up"], w_hi, w_lo)
            split_weights(m, a["router1"], r_hi, r_lo)
            gates = m.sbuf("gates1", [P, NT * E], F32, c)
            route(m, FS, r_hi[:], r_lo[:], a["router1_bias"], a["before"], gates)
            mix_gelu(m, FS, w_hi, w_lo, a["gelu_b1"], a["gelu_down"], a["gelu_b2"], gates, m.H)
        stored = m.sem("stored")
        with nc.Block() as block:
            @block.sync
            def _(sp):
                sp.dma_start(out.rearrange("b (t p) c -> p (b t) c", p=P), tiles(m.H)).then_inc(stored, 16)
                sp.wait_ge(stored, 16)


def arrays(v):
    g = {k: np.asarray(x) for k, x in v.items()}
    l0, ff = (lambda k: g["L0_attn_" + k]), (lambda k: g["L0_ffn_" + k])
    eye = np.eye(P, dtype=np.float32)
    row = np.arange(P)
    iota = row[:, None].astype(np.float32)
    iota[0] = -1
    table, turns, masks = relative_constants()
    rows, biases, pos = relative_weights(l0("Wq"), l0("bq"), l0("Wk"), l0("bk"), l0("Wpos"), l0("u_bias"), l0("v_bias"))
    zero_row = np.zeros((1, D), np.float32)

    half = 8
    inv = 1.0 / 10000.0 ** (np.arange(0, 16, 2, dtype=np.float32) / 16)
    emb = np.concatenate([np.outer(np.arange(S, dtype=np.float32), inv)] * 2, -1).T
    sign = np.where(np.arange(16) < half, -1, 1)[:, None]
    rope = np.concatenate([np.tile(np.cos(emb), (8, 1)), np.tile(np.sin(emb) * sign, (8, 1))], 1).astype(np.float32)
    causal = []
    for h in range(4):
        q = ff("wq")[16 * h:16 * h + 16].T
        k = ff("wk")[16 * (h // 2):16 * (h // 2) + 16].T
        swap = lambda w: np.concatenate([w[:, half:], w[:, :half]], 1)
        causal.append(np.concatenate([q] * 4 + [k] * 4 + [swap(q)] * 4 + [swap(k)] * 4, 1))
    zeros22 = np.zeros((D, D - REST), np.float32)
    gated = []
    for e in range(E):
        w1, w3 = ff("w1")[e].T, ff("w3")[e].T
        gated += [w1[:, :P], w3[:, :P], w1[:, P:], zeros22, w3[:, P:]]
    WQ, WK = g["L1_attn_WQ"], g["L1_attn_WK"]
    wide = [np.concatenate([WQ[:, h * D:(h + 1) * D]] * 2 + [WK[:, h * D:(h + 1) * D]] * 2, 1) for h in range(8)]
    e_row = np.arange(E)
    out = dict(
        tokens=g["x"], token_W=g["L0_tok_token_W"], pe_rows=g["L0_tok_pe"][:2].reshape(1, 2 * D), iota=iota,
        ident=eye, split=split_columns(), join32=np.tile(eye[:32, :32], (4, 1)), join64=np.tile(eye[:64, :64], (2, 1)),
        causal_mask=np.concatenate([np.where(row[:, None] > np.arange(BANK)[None] - (BANK - P), NEG, 0),
                                    np.where(row[None, :] > row[:, None], NEG, 0)], 1).astype(np.float32),
        ln_gamma=l0("ln_gamma"), ln_beta=l0("ln_beta"), rel_v=np.concatenate([l0("Wv"), l0("bv")[None], zero_row]),
        rel_rows=rows, rel_bias=biases, rel_pos=pos, pe_table=table, turns=turns, rel_masks=masks,
        rel_out=np.concatenate([l0("Wout"), l0("bout")[None]]),
        ln1_w=ff("ln1_w"), ln2_w=ff("ln2_w"), causal_qk=np.stack(causal * B), causal_v=ff("wv").T, rope_table=rope,
        causal_out=ff("wo").T, router0=ff("router_w").T, gated_up=np.concatenate(gated, 1),
        gated_down=ff("w2").transpose(2, 0, 1).reshape(HID, E * D),
        before=(e_row[None, :] < e_row[:, None]).astype(np.float32).reshape(E * E),
        wide_qk=np.stack(wide * B), wide_v=g["L1_attn_WV"], wide_out=g["L1_attn_Wout"], wide_bout=g["L1_attn_bout"],
        gamma1=g["L1_ffn_gamma"], beta1=g["L1_ffn_beta"], router1=g["L1_ffn_Wr"], router1_bias=g["L1_ffn_br"],
        gelu_up=g["L1_ffn_W1"].transpose(1, 0, 2).reshape(D, E * P), gelu_b1=g["L1_ffn_b1"].T,
        gelu_down=g["L1_ffn_W2"], gelu_b2=g["L1_ffn_b2"].reshape(E * D))
    return {k: np.ascontiguousarray(x) for k, x in out.items()}


def kernel(**inputs):
    import concourse.bacc as bacc
    from concourse.bass_utils import run_bass_kernel_spmd

    nc = bacc.Bacc("TRN2", target_bir_lowering=False, num_devices=1)
    sent, args = {}, {}
    for name, x in arrays(inputs).items():
        sent[name + "_dram"] = x
        args[name] = nc.dram_tensor(name + "_dram", x.shape, mybir.dt.from_np(x.dtype), kind="ExternalInput").ap()
    out = nc.dram_tensor("out_dram", (B, S, D), F32, kind="ExternalOutput").ap()
    tower(nc, args, out)
    result = run_bass_kernel_spmd(nc, [sent], core_ids=[0])
    return result.results[0]["out_dram"]
```
